# Optimizing a Trainium2 kernel written in Bass

```python
import numpy as np
import jax
import jax.numpy as jnp

def _softmax(x, axis=-1):
    return jax.nn.softmax(x, axis=axis)

def _gelu(x):
    return jax.nn.gelu(x, approximate=True)

def _silu(x):
    return jax.nn.silu(x)

def _sigmoid(x):
    return jax.nn.sigmoid(x)

def _layernorm(x, axis=-1, eps=1e-05):
    m = jnp.mean(x, axis=axis, keepdims=True)
    v = jnp.var(x, axis=axis, keepdims=True)
    return (x - m) / jnp.sqrt(v + eps)

def _scatter_add(tgt, idx, src, axis=0):
    return tgt.at[idx].add(src)

def _segment_sum(src, seg, n):
    return jax.ops.segment_sum(src, seg, n)
kernel_name = 'mk_gnn_resnorm_d2_gnn_r8_455832'

def setup_inputs(seed: int=0):
    np.random.seed(seed)
    _w = jnp.asarray

    def _rec_inputs():
        import jax
        import jax.numpy as jnp
        _gk = jax.random.key(seed)
        x = -0.000202 + 1 * jax.random.normal(jax.random.fold_in(_gk, 1), (6250, 128), jnp.float32)
        _s = jax.random.randint(jax.random.fold_in(_gk, 2), (100000,), 0, 6250, jnp.int32)
        _d = jax.random.randint(jax.random.fold_in(_gk, 3), (100000,), 0, 6250, jnp.int32)
        _loop = jnp.arange(6250, dtype=jnp.int32)
        src = jnp.concatenate([_s, _d, _loop])
        dst = jnp.concatenate([_d, _s, _loop])
        _o = jnp.argsort(dst, stable=True)
        src = src[_o]
        dst = dst[_o]
        edge_type_64 = jax.random.randint(jax.random.fold_in(_gk, 13), (206250,), 0, 64, jnp.int32)
        edge_type_8 = jax.random.randint(jax.random.fold_in(_gk, 14), (206250,), 0, 8, jnp.int32)
        edge_weight1 = jax.random.uniform(jax.random.fold_in(_gk, 15), (206250, 1), jnp.float32, 0.0, 0.999998)
        return (x, src, dst, edge_type_64, edge_type_8, edge_weight1)
    x, src, dst, edge_type_64, edge_type_8, edge_weight1 = _rec_inputs()

    def _L0_gnn_setup():
        import jax, jax.numpy as jnp
        import numpy as np
        N, E, D_IN, D_OUT, R = (6250, 100000, 128, 128, 8)
        key = jax.random.key(seed)
        ks = jax.random.split(key, 6)
        x = jax.random.normal(ks[0], (N, D_IN), dtype=jnp.float32)
        W_rel = jax.random.normal(ks[1], (R, D_IN, D_OUT), dtype=jnp.float32) * (1.0 / np.sqrt(D_IN))
        W_self_w = jax.random.normal(ks[2], (D_OUT, D_IN), dtype=jnp.float32) * (1.0 / np.sqrt(D_IN))
        W_self_b = jax.random.normal(ks[3], (D_OUT,), dtype=jnp.float32) * 0.01
        edge_index = jax.random.randint(ks[4], (2, E), 0, N, dtype=jnp.int32)
        edge_type = jax.random.randint(ks[5], (E,), 0, R, dtype=jnp.int32)
        return {'x': x, 'W_rel': W_rel, 'W_self_w': W_self_w, 'W_self_b': W_self_b, 'edge_index': edge_index, 'edge_type': edge_type}
    _L0_gnn_all = _L0_gnn_setup()
    _L0_gnn_in = {k: v for k, v in _L0_gnn_all.items() if k in ('W_rel', 'W_self_w', 'W_self_b')}
    del _L0_gnn_all

    def _L1_gnn_setup():
        import jax, jax.numpy as jnp
        import numpy as np
        N, E, IN, OUT, R, B = (2500, 80000, 128, 128, 64, 16)
        key = jax.random.key(seed)
        ks = jax.random.split(key, 9)
        xav_w = float(np.sqrt(2.0 / (IN + OUT)))
        xav_c = float(np.sqrt(2.0 / (R + B)))
        return {'x': jax.random.normal(ks[0], (N, IN), jnp.float32), 'weight': jax.random.normal(ks[1], (B, IN, OUT), jnp.float32) * xav_w, 'w_comp': jax.random.normal(ks[2], (R, B), jnp.float32) * xav_c, 'h_bias': jnp.zeros((OUT,), jnp.float32), 'loop_weight': jax.random.normal(ks[3], (IN, OUT), jnp.float32) * xav_w, 'norm': jax.random.uniform(ks[4], (E, 1), jnp.float32), 'src': jax.random.randint(ks[5], (E,), 0, N, jnp.int32), 'dst': jax.random.randint(ks[6], (E,), 0, N, jnp.int32), 'etypes': jax.random.randint(ks[7], (E,), 0, R, jnp.int32)}
    _L1_gnn_all = _L1_gnn_setup()
    _L1_gnn_in = {k: v for k, v in _L1_gnn_all.items() if k in ('weight', 'w_comp', 'h_bias', 'loop_weight')}
    del _L1_gnn_all
    return {'x': x, 'src': src, 'dst': dst, 'edge_type_64': edge_type_64, 'edge_type_8': edge_type_8, 'edge_weight1': edge_weight1, 'L0_gnn_W_rel': _L0_gnn_in['W_rel'], 'L0_gnn_W_self_w': _L0_gnn_in['W_self_w'], 'L0_gnn_W_self_b': _L0_gnn_in['W_self_b'], 'L1_gnn_weight': _L1_gnn_in['weight'], 'L1_gnn_w_comp': _L1_gnn_in['w_comp'], 'L1_gnn_h_bias': _L1_gnn_in['h_bias'], 'L1_gnn_loop_weight': _L1_gnn_in['loop_weight']}

def reference(x, src, dst, edge_type_64, edge_type_8, edge_weight1, L0_gnn_W_rel, L0_gnn_W_self_w, L0_gnn_W_self_b, L1_gnn_weight, L1_gnn_w_comp, L1_gnn_h_bias, L1_gnn_loop_weight):
    import jax
    import jax.numpy as jnp

    def _L0_gnn_ref(x, W_rel, W_self_w, W_self_b, edge_index, edge_type):
        import jax, jax.numpy as jnp
        import numpy as np
        N, E, D_IN, D_OUT, R = (6250, 100000, 128, 128, 8)
        n = x.shape[0]
        out = x @ W_self_w.T + W_self_b
        src = edge_index[0]
        dst = edge_index[1]
        h = jnp.einsum('nd,rdo->rno', x, W_rel)
        msg = h[edge_type, src]
        agg = jax.ops.segment_sum(msg, dst, num_segments=n)
        deg = jax.ops.segment_sum(jnp.ones_like(dst, dtype=x.dtype), dst, num_segments=n)
        deg = jnp.maximum(deg, 1.0)[:, None]
        out = jax.nn.relu(out + agg / deg)
        return out

    def _L1_gnn_ref(x, weight, w_comp, h_bias, loop_weight, norm, src, dst, etypes):
        import jax, jax.numpy as jnp
        import numpy as np
        N, E, IN, OUT, R, B = (2500, 80000, 128, 128, 64, 16)
        W_rel = jnp.einsum('rb,bio->rio', w_comp, weight)
        h_all = jnp.einsum('ni,rio->nro', x, W_rel)
        msg = h_all[src, etypes] * norm
        agg = jax.ops.segment_sum(msg, dst, num_segments=x.shape[0])
        out = agg + h_bias + x @ loop_weight
        return jax.nn.relu(out)
    edge_index = jnp.stack([src, dst])
    x = _layernorm(x + _L0_gnn_ref(x, L0_gnn_W_rel, L0_gnn_W_self_w, L0_gnn_W_self_b, edge_index, edge_type_8), axis=-1)
    x = _layernorm(x + _L1_gnn_ref(x, L1_gnn_weight, L1_gnn_w_comp, L1_gnn_h_bias, L1_gnn_loop_weight, edge_weight1, src, dst, edge_type_64), axis=-1)
    return x

_drawn_inputs = setup_inputs


def setup_inputs(seed=0):
    import zlib

    import numpy as np

    out = dict(_drawn_inputs(seed))
    spreads = {'L1_gnn_h_bias': (0.0, 0.1)}
    factors = {'L0_gnn_W_self_b': 7.423}
    for name, (base, spread) in spreads.items():
        noise = np.random.default_rng([zlib.crc32(name.encode()), seed]).standard_normal(out[name].shape)
        drawn = base * np.exp(spread * noise) if base else spread * noise
        out[name] = jnp.asarray(drawn.astype(out[name].dtype))
    for name, factor in factors.items():
        out[name] = (out[name] * factor).astype(out[name].dtype)
    return out
```

```python
from contextlib import ExitStack

import concourse.bass as bass
from concourse import mybir

F32 = mybir.dt.float32
BF16 = mybir.dt.bfloat16
I32 = mybir.dt.int32
U32 = mybir.dt.uint32
ALU = mybir.AluOpType
ACT = mybir.ActivationFunctionType
AX = mybir.AxisListType

P = 128
GROUP = 8
SPAN = 16
STEP = 8
WINDOW = 64
BANK = 512
FAR = 8192
EPS = 1e-5
BATCH = 4


def two_layer_gnn(nc, x, src, dst, type64, type8, weight, w_rel, w_self, b_self,
                  w_basis, w_comp, h_bias, w_loop, out):
    nodes, feat = x.shape
    edges = src.shape[0]
    types0 = w_rel.shape[0]
    types1, bases = w_comp.shape
    assert feat == P and nodes < FAR
    chunks = -(-edges // P)
    groups = -(-chunks // (2 * GROUP)) * 2
    cols = groups * GROUP
    tiles = -(-cols // P)
    full_tiles = edges // (P * P)
    rest_rows = edges // P - full_tiles * P
    rest = edges - (edges // P) * P
    pad_nodes = -(-(nodes + WINDOW) // P) * P
    dump = nodes + WINDOW - 1
    assert full_tiles == tiles - 1 and rest > 0
    GE = GROUP * P
    pairs = groups // 2
    NB = BATCH * P
    full_batches = nodes // NB
    last_nodes = nodes - full_batches * NB
    assert full_batches % 2 == 0 and 0 < last_nodes <= P

    ctx = ExitStack()
    with ctx:
        def sb(name, shape, dt=F32):
            return ctx.enter_context(nc.sbuf_tensor(name, shape, dt))

        def sem(name):
            return ctx.enter_context(nc.semaphore(name))

        x1 = nc.dram_tensor("x1", (nodes, feat), F32, kind="Internal").ap()
        plan_lin = nc.dram_tensor("plan_lin", (2, tiles * P), F32, kind="Internal").ap()
        dst_lin = nc.dram_tensor("dst_lin", (tiles * P * P,), I32, kind="Internal").ap()
        type_lin = nc.dram_tensor("type_lin", (tiles * P * P,), BF16, kind="Internal").ap()

        src_nat = sb("src_nat", [P, tiles, P], I32)
        dst_nat = sb("dst_nat", [P, tiles, P], I32)
        type_nat = sb("type_nat", [P, tiles, P], I32)
        weight_nat = sb("weight_nat", [P, tiles, P])
        src_f = sb("src_f", [P, tiles, P])
        dst_f = sb("dst_f", [P, tiles, P])
        src_col = sb("src_col", [P, tiles * P])
        rel_col = sb("rel_col", [P, tiles * P])
        type_col = sb("type_col", [P, tiles * P])
        weight_col = sb("weight_col", [P, tiles * P])
        low = sb("low", [P, tiles])
        low_i = sb("low_i", [P, tiles], I32)
        base8_i = sb("base8_i", [P, tiles], I32)
        high = sb("high", [P, tiles])
        base_span = sb("base_span", [P, 2 * tiles])
        base8, span = base_span[:, 0:tiles], base_span[:, tiles:2 * tiles]
        base_span_t = sb("base_span_t", [2 * tiles, P])
        group_base = sb("group_base", [1, groups])
        group_node = sb("group_node", [1, groups], I32)
        offset = sb("offset", [1, cols], I32)
        worst = sb("worst", [1, 4])
        general = sb("general", [1, 1], I32)
        iota_i = sb("iota_i", [P, P], I32)
        lane_i = sb("lane_i", [P, 1], I32)
        iota_f = sb("iota_f", [P, P])
        lane_f = sb("lane_f", [P, 1])
        ident = sb("ident", [P, P])
        ones_b = sb("ones_b", [P, P], BF16)
        zeros_b = sb("zeros_b", [P, BANK], BF16)
        w0 = sb("w0", [P, types0, P])
        w1 = sb("w1", [P, bases, P])
        w_self_nat = sb("w_self_nat", [P, P])
        w_node = [sb("w_self_t", [P, P]), sb("w_loop_sb", [P, P])]
        bias = [sb("bias0", [P, 1]), sb("bias1", [P, 1])]
        comp = sb("comp", [P, bases])
        comp_left = sb("comp_left", [P, 2, bases])
        comp_part = sb("comp_part", [P, 3, bases], BF16)
        index = [sb(f"index{s}", [P, GROUP], U32) for s in range(2)]
        rows = [sb(f"rows{s}", [P, GROUP, P]) for s in range(2)]
        onehot = [sb(f"onehot{s}", [P, GROUP, SPAN], BF16) for s in range(2)]
        coef = [sb(f"coef{s}", [P, GROUP, bases]) for s in range(2)]
        sel = [sb(f"sel{s}", [P, GROUP * SPAN * bases]) for s in range(2)]
        base_row, span_row = [a[0:1, 0:tiles * P] for a in sel]
        type_row = [sb(f"type_row{s}", [1, GE], BF16) for s in range(2)]
        type_hot = sb("type_hot", [P, GE], BF16)
        win_sb = [sb(f"win_sb{s}", [P, bases * WINDOW]) for s in range(2)]
        one_chunk = sb("one_chunk", [P, P])
        agg = sb("agg", [P, pad_nodes])
        deg = sb("deg", [P, pad_nodes])
        x_in = [sb(f"x_in{s}", [P, BATCH, P]) for s in range(2)]
        x_t = sb("x_t", [P, NB])
        act_t = sb("act_t", [P, NB])
        y = [sb(f"y{s}", [P, BATCH, P]) for s in range(2)]
        stats = [sb(f"stats{s}", [P, BATCH, 6]) for s in range(2)]
        moments = [sb(f"moments{s}", [P, BATCH, 2]) for s in range(2)]
        std = [sb(f"std{s}", [P, BATCH]) for s in range(2)]
        eps = sb("eps", [P, 1])
        rstd = [sb(f"rstd{s}", [P, BATCH]) for s in range(2)]
        shift = [sb(f"shift{s}", [P, BATCH]) for s in range(2)]
        y_out = [sb(f"y_out{s}", [P, BATCH, P]) for s in range(2)]

        bank = [ctx.enter_context(nc.psum_tensor(f"bank{i}", [P, 2 * BANK], F32)) for i in range(2)]
        bank += [ctx.enter_context(nc.psum_tensor(f"bank{i}", [P, BANK], F32)) for i in range(2, 6)]
        win_ps, prod_ps, coef_ps = bank[0:2], bank[2], bank[5]
        deg_ps = bank[3:5]

        def by_layer(name):
            return [sem(f"{name}_{l}") for l in range(2)]

        def by_slot(name):
            return [sem(f"{name}_{s}") for s in range(2)]

        src_in, dst_in, type8_in, type64_in = sem("src_in"), sem("dst_in"), sem("type8_in"), sem("type64_in")
        weight_in, w_in = sem("weight_in"), sem("w_in")
        pads_set, consts_set, sums_zeroed = sem("pads_set"), sem("consts_set"), sem("sums_zeroed")
        prep = sem("prep")
        ident_ready, src_float, spans_ready = sem("ident_ready"), sem("src_float"), sem("spans_ready")
        spans_turned, spans_copied = sem("spans_turned"), sem("spans_copied")
        rel_ready, dst_clamped, types_float = sem("rel_ready"), sem("dst_clamped"), sem("types_float")
        types64_float, comp_ready = sem("types64_float"), sem("comp_ready")
        turned, cols_copied = sem("turned"), sem("cols_copied")
        w_self_turned, w_self_copied = sem("w_self_turned"), sem("w_self_copied")
        lin_out, lin_in, dst_out, type_out = sem("lin_out"), sem("lin_in"), sem("dst_out"), sem("type_out")
        plan_ready, cols_ready = sem("plan_ready"), sem("cols_ready")
        idx_staged, hots_ready, sel_ready = by_layer("idx_staged"), by_layer("hots_ready"), by_layer("sel_ready")
        rows_landed = [by_slot(f"rows_landed_{l}") for l in range(2)]
        sums_done, win_copied, prod_done = by_layer("sums_done"), by_layer("win_copied"), by_layer("prod_done")
        evacuated, stream_done = by_layer("evacuated"), by_layer("stream_done")
        pool_paced, scalar_paced, vector_paced = sem("pool_paced"), sem("scalar_paced"), sem("vector_paced")
        type_row_in = by_slot("type_row_in")
        types_spread, type_hot_ready, coef_summed = sem("types_spread"), sem("type_hot_ready"), sem("coef_summed")
        agg_zeroed = sem("agg_zeroed")
        g_coef, g_rows, g_sel, g_sums = by_layer("g_coef"), by_layer("g_rows"), by_layer("g_sel"), by_layer("g_sums")
        g_copied, g_prod, g_added = by_layer("g_copied"), by_layer("g_prod"), by_layer("g_added")
        x_in_landed = [by_slot(f"x_in_landed_{l}") for l in range(2)]
        x_turned, x_t_copied, mean_step = by_layer("x_turned"), by_layer("x_t_copied"), by_layer("mean_step")
        node_summed, act_ready, act_turned = by_layer("node_summed"), by_layer("act_ready"), by_layer("act_turned")
        node_step, rstd_ready, normed = by_layer("node_step"), by_layer("rstd_ready"), by_layer("normed")
        moments_ready, std_ready, inverted = by_layer("moments_ready"), by_layer("std_ready"), by_layer("inverted")
        stored = [by_slot(f"stored_{l}") for l in range(2)]

        block = ctx.enter_context(nc.Block())

        fan = [types0, bases]
        weights = [w0, w1]
        EV = [2, 1]
        HALF = P // 2

        def known(g):
            return isinstance(g, int)

        def over_groups(eng, step):
            for s in range(2):
                step(s, s, 0)
            with eng.Fori(1, pairs - 1) as k:
                for s in range(2):
                    step(2 * k + s, s, k)
            for s in range(2):
                step(groups - 2 + s, s, pairs - 1)

        def over_batches(eng, step, end=None):
            for s in range(2):
                step(s, s, 0, NB)
            for s in range(2):
                step(2 + s, s, 1, NB)
            with eng.Fori(2, full_batches // 2) as k:
                for s in range(2):
                    step(2 * k + s, s, k, NB)
            step(full_batches, 0, full_batches // 2, last_nodes)

        def span_of(b, n):
            return bass.ds(b * NB, n)

        def parts_of(n):
            return [(j, min(P, n - j * P)) for j in range(-(-n // P))]

        def all_stored(eng, l):
            for s in range(2):
                eng.wait_ge(stored[l][s], 16 * (full_batches // 2 + 1 - s))

        def paths(eng, fast, general_path):
            verdict = eng.value_load(general[0:1, 0:1], min_val=0, max_val=2)
            with eng.If(verdict < 1):
                fast()
                eng.nop()
            with eng.Else():
                general_path()
                eng.nop()

        @block.sync
        def _(sp):
            def load_edges(a, nat, landed, pads):
                flat = a if len(a.shape) == 1 else a.rearrange("e o -> (e o)")
                n = full_tiles * P * P
                sp.dma_start(nat[:, 0:full_tiles, :],
                             flat[0:n].rearrange("(j p e) -> p j e", p=P, e=P)).then_inc(landed, 16)
                sp.wait_ge(pads_set, pads)
                sp.dma_start(nat[0:rest_rows, full_tiles, :],
                             flat[n:n + rest_rows * P].rearrange("(p e) -> p e", e=P)).then_inc(landed, 16)
                sp.dma_start(nat[rest_rows:rest_rows + 1, full_tiles, 0:rest],
                             flat[n + rest_rows * P:edges].rearrange("(p e) -> p e", e=rest)).then_inc(landed, 16)

            load_edges(src, src_nat, src_in, 1)
            load_edges(dst, dst_nat, dst_in, 2)
            load_edges(type8, type_nat, type8_in, 3)
            load_edges(weight, weight_nat, weight_in, 4)
            sp.dma_start(w_self_nat[:, :], w_self).then_inc(w_in, 16)
            sp.dma_start(w0[:, :, :], w_rel.rearrange("r i o -> i r o")).then_inc(w_in, 16)
            sp.wait_ge(spans_copied, 1)
            sp.dma_start(plan_lin.rearrange("o (j p) -> (o j) p", p=P), base_span_t[:, :]).then_inc(lin_out, 16)
            sp.wait_ge(lin_out, 16)
            sp.dma_start(base_row, plan_lin[0:1, :]).then_inc(lin_in, 16)
            sp.dma_start(span_row, plan_lin[1:2, :]).then_inc(lin_in, 16)

            sp.dma_start(w1[:, :, :], w_basis.rearrange("r i o -> i r o")).then_inc(w_in, 16)
            sp.dma_start(w_node[1][:, :], w_loop).then_inc(w_in, 16)
            sp.dma_start(bias[0][:, :], b_self.rearrange("(o c) -> o c", c=1)).then_inc(w_in, 16)
            sp.dma_start(bias[1][:, :], h_bias.rearrange("(o c) -> o c", c=1)).then_inc(w_in, 16)
            sp.wait_ge(pads_set, 5)
            sp.dma_start(comp[0:types1, :], w_comp).then_inc(w_in, 16)
            sp.wait_ge(dst_clamped, 1)
            sp.dma_start(dst_lin.rearrange("(j p e) -> p j e", p=P, e=P), src_nat[:, :, :]).then_inc(dst_out, 16)
            sp.wait_ge(types_float, 1)
            load_edges(type64, type_nat, type64_in, 5)
            sp.wait_ge(types64_float, 1)
            sp.dma_start(type_lin.rearrange("(j p e) -> p j e", p=P, e=P),
                         src_f[:, :, :].bitcast(BF16)[:, :, 0:P]).then_inc(type_out, 16)

            def nodes_in_and_out(l):
                source, target = [x, x1][l], [x1, out][l]

                def store(b, s, n):
                    sp.wait_ge(normed[l], b + 1)
                    if n == NB:
                        sp.dma_start(target[span_of(b, n), :].rearrange("(j p) f -> p j f", p=P),
                                     y_out[s][:, :, :]).then_inc(stored[l][s], 16)
                    else:
                        sp.dma_start(target[span_of(b, n), :], y_out[s][0:n, 0, :]).then_inc(stored[l][s], 16)

                def step(b, s, k, n):
                    if not (known(b) and b < 2):
                        sp.wait_ge(moments_ready[l], b - 1)
                    if n == NB:
                        sp.dma_start(x_in[s][:, :, :],
                                     source[span_of(b, n), :].rearrange("(j p) f -> p j f", p=P)
                                     ).then_inc(x_in_landed[l][s], 16)
                    else:
                        sp.dma_start(x_in[s][0:n, 0, :], source[span_of(b, n), :]
                                     ).then_inc(x_in_landed[l][s], 16)
                    if not (known(b) and b < 3):
                        store(b - 3, 1 - s, NB)
                    if n != NB:
                        store(b - 2, s, NB)
                        store(b - 1, 1 - s, NB)
                        store(b, s, n)
                over_batches(sp, step)

            nodes_in_and_out(0)

            def load_types(g, s, k):
                if not (known(g) and g < 2):
                    sp.wait_ge(types_spread, g - 1)
                sp.dma_start(type_row[s][:, :], type_lin[bass.ds(g * GE, GE)].rearrange("(o e) -> o e", o=1)
                             ).then_inc(type_row_in[s], 16)
            sp.wait_ge(type_out, 16)
            over_groups(sp, load_types)
            all_stored(sp, 0)
            nodes_in_and_out(1)
            all_stored(sp, 1)
            sp.wait_ge(dst_out, 16)

        @block.gpsimd
        def _(gp):
            gp.memset(src_nat[:, full_tiles, :], 0).then_inc(pads_set, 1)
            gp.memset(dst_nat[:, full_tiles, :], FAR).then_inc(pads_set, 1)
            gp.memset(type_nat[:, full_tiles, :], types0).then_inc(pads_set, 1)
            gp.memset(weight_nat[:, full_tiles, :], 0.0).then_inc(pads_set, 1)
            gp.memset(comp[:, :], 0.0).then_inc(pads_set, 1)
            gp.iota(iota_i[:, :], pattern=[[1, P]], base=0, channel_multiplier=0).then_inc(consts_set, 1)
            gp.iota(lane_i[:, :], pattern=[[1, 1]], base=0, channel_multiplier=1).then_inc(consts_set, 1)
            gp.memset(agg[:, :], 0.0).then_inc(sums_zeroed, 1)
            gp.memset(deg[:, :], 0.0).then_inc(sums_zeroed, 1)

            for l in range(2):
                table = [x, x1][l]
                if l:
                    all_stored(gp, 0)

                def gather(g, s, k):
                    gp.wait_ge(idx_staged[l], g + 1)
                    gp.sem_inc(pool_paced, 1)
                    for i in range(GROUP):
                        gp.indirect_dma_start(rows[s][:, i, :], None, table,
                                              bass.IndirectOffsetOnAxis(index[s][:, i:i + 1], 0)
                                              ).then_inc(rows_landed[l][s], 16)
                over_groups(gp, gather)

        @block.scalar
        def _(sc):
            n = 0
            for col in (src_col, rel_col, type_col, weight_col):
                for j in range(0, tiles, 4):
                    w = min(4, tiles - j) * P
                    n += 1
                    sc.wait_ge(turned, n)
                    sc.copy(col[:, j * P:j * P + w], deg_ps[n % 2][:, 0:w]).then_inc(cols_copied, 1)
                    if n == -(-tiles // 4):
                        sc.wait_ge(spans_turned, 1)
                        sc.copy(base_span_t[:, :], coef_ps[0:2 * tiles, 0:P]).then_inc(spans_copied, 1)
                    if n == 1:
                        sc.wait_ge(cols_copied, 1)
                        for s in range(2):
                            sc.copy(index[s][:, :], src_col[:, s * GROUP:(s + 1) * GROUP]).then_inc(idx_staged[0], 1)
            sc.wait_ge(w_self_turned, 1)
            sc.copy(w_node[0][:, :], coef_ps[:, 0:P]).then_inc(w_self_copied, 1)
            sc.wait_ge(cols_copied, n)
            sc.wait_ge(plan_ready, 3)

            for l in range(2):
                r = fan[l]

                def stage(g, s):
                    sc.copy(index[s][:, :], src_col[:, bass.ds(g * GROUP, GROUP)]).then_inc(idx_staged[l], 1)

                if l:
                    for s in range(2):
                        stage(s, s)

                def fast():
                    def step(g, s, k):
                        sc.wait_ge(sums_done[l], g + 1)
                        sc.copy(win_sb[s][:, 0:WINDOW * r].rearrange("p (r w) -> p r w", r=r),
                                win_ps[s][:, 0:WINDOW * r].rearrange("p (w r) -> p r w", r=r)
                                ).then_inc(win_copied[l], 1)
                        if not (known(g) and g >= groups - 2):
                            stage(g + 2, s)
                    over_groups(sc, step)

                def general_path():
                    with sc.Fori(0, pairs) as k:
                        for s in range(2):
                            g = 2 * k + s
                            sc.wait_ge(rows_landed[l][s], (k + 1) * (16 * GROUP))
                            sc.sem_inc(scalar_paced, 1)
                            with sc.Fori(0, GROUP) as i:
                                for h in range(2):
                                    u = (g * GROUP + i) * 2 + h
                                    if h == 0:
                                        sc.wait_ge(g_sums[l], u + 1)
                                        sc.sem_inc(scalar_paced, 1)
                                        sc.copy(one_chunk[:, :], rows[s][:, bass.ds(i, 1), :].rearrange(
                                            "p o f -> p (o f)")).then_inc(g_rows[l], 1)
                                    sc.wait_ge(g_sums[l], u + 2)
                                    sc.copy(win_sb[0][:, 0:HALF * r].rearrange("p (r w) -> p r w", r=r),
                                            win_ps[0][:, 0:HALF * r].rearrange("p (w r) -> p r w", r=r)
                                            ).then_inc(g_copied[l], 1)
                            stage(g + 2, s)

                paths(sc, fast, general_path)

                def norm(b, s, k, n):
                    sc.wait_ge(rstd_ready[l], b + 1)
                    if not (known(b) and b < 2):
                        sc.wait_ge(stored[l][s], k * 16)
                    for j, m in parts_of(n):
                        ins = sc.activation(y_out[s][0:m, j, :], y[s][0:m, j, :], ACT.Identity,
                                            bias=shift[s][0:m, j:j + 1], scale=rstd[s][0:m, j:j + 1])
                    ins.then_inc(normed[l], 1)

                def deviation(b, s, n):
                    sc.wait_ge(moments_ready[l], b + 1)
                    m, c = min(n, P), len(parts_of(n))
                    sc.activation(std[s][0:m, 0:c], moments[s][0:m, 0:c, 1], ACT.Sqrt,
                                  bias=eps[0:m, 0:1]).then_inc(std_ready[l], 1)

                def node_step_scalar(b, s, k, n):
                    sc.wait_ge(x_turned[l], b + 1)
                    sc.copy(x_t[:, 0:n], win_ps[s][:, 0:n]).then_inc(x_t_copied[l], 1)
                    sc.wait_ge(node_summed[l], b + 1)
                    sc.activation(act_t[:, 0:n], win_ps[s][:, BANK:BANK + n], ACT.Relu,
                                  bias=bias[l][:, 0:1]).then_inc(act_ready[l], 1)
                    if not (known(b) and b < 1):
                        deviation(b - 1, 1 - s, NB)
                    if not (known(b) and b < 2):
                        norm(b - 2, s, k - 1, NB)
                    if n != NB:
                        deviation(b, s, n)
                        norm(b - 1, 1 - s, k - 1, NB)
                        norm(b, s, k, n)
                sc.wait_ge(stream_done[l], 1)
                sc.wait_ge(w_in, 16 * 7)
                over_batches(sc, node_step_scalar)

        @block.tensor
        def _(pe):
            n = 0
            pe.wait_ge(ident_ready, 1)
            for nat, ready, amount in ((src_f, src_float, 1), (dst_f, rel_ready, 1),
                                       (src_f, types_float, 1), (weight_nat, weight_in, 48)):
                pe.wait_ge(ready, amount)
                for j in range(0, tiles, 4):
                    w = min(4, tiles - j)
                    n += 1
                    if n > 2:
                        pe.wait_ge(cols_copied, n - 2)
                    for i in range(w):
                        ins = pe.transpose(deg_ps[n % 2][:, i * P:(i + 1) * P], nat[:, j + i, :], ident[:, :])
                    ins.then_inc(turned, 1)
                if nat is src_f and ready is src_float:
                    pe.wait_ge(spans_ready, 1)
                    pe.transpose(coef_ps[0:2 * tiles, 0:P], base_span[:, :], ident[:, :]).then_inc(spans_turned, 1)
            pe.wait_ge(w_in, 16 * 7)
            pe.wait_ge(spans_copied, 1)
            pe.transpose(coef_ps[:, 0:P], w_self_nat[:, :], ident[:, :]).then_inc(w_self_turned, 1)
            pe.wait_ge(w_self_copied, 1)
            pe.wait_ge(cols_copied, n)
            pe.wait_ge(plan_ready, 3)
            pe.wait_ge(comp_ready, 1)
            shifts = [pe.alloc_register(f"shift{i}") for i in range(GROUP)]

            def spread_types(g, s, k):
                pe.wait_ge(type_row_in[s], (k + 1) * 16)
                for b in range(2):
                    ins = pe.matmul(deg_ps[b][:, :], ones_b[0:1, :], type_row[s][:, b * BANK:(b + 1) * BANK],
                                    start=True, stop=True)
                ins.then_inc(types_spread, 1)

            def sum_coef(g):
                pe.wait_ge(type_hot_ready, g + 1)
                for i in range(GROUP):
                    for part in range(3):
                        ins = pe.matmul(coef_ps[:, i * bases:(i + 1) * bases], type_hot[:, i * P:(i + 1) * P],
                                        comp_part[:, part, :], start=part == 0, stop=part == 2)
                ins.then_inc(coef_summed, 1)

            for l in range(2):
                r = fan[l]

                def sums(g, s, k):
                    if not (known(g) and g < 2):
                        pe.wait_ge(win_copied[l], g - 1)
                        if l == 0:
                            pe.wait_ge(evacuated[l], (g - 1) * EV[l])
                    for b in range(WINDOW * r // BANK):
                        pe.matmul(win_ps[s][:, b * BANK:(b + 1) * BANK], zeros_b[:, 0:P], zeros_b[:, :],
                                  start=True, stop=False, skip_group_check=True)
                    if l == 0:
                        pe.matmul(deg_ps[s][:, 0:WINDOW], zeros_b[:, 0:P], zeros_b[:, 0:WINDOW],
                                  start=True, stop=False, skip_group_check=True)
                    pe.load(shifts, offset[0:1, bass.ds(g * GROUP, GROUP)])
                    pe.wait_ge(sel_ready[l], g + 1)
                    pe.wait_ge(rows_landed[l][s], (k + 1) * (16 * GROUP))
                    for i in range(GROUP):
                        first = pe.snap(shifts[i], min_val=0, max_val=WINDOW - SPAN)
                        for h in range(SPAN * r // P):
                            ins = pe.matmul(win_ps[s][:, bass.ds(first * r + h * P, P)], rows[s][:, i, :],
                                            sel[s][:, i * SPAN * r + h * P:i * SPAN * r + (h + 1) * P],
                                            start=False, stop=True, skip_group_check=True)
                        if l == 0:
                            ins = pe.matmul(deg_ps[s][:, bass.ds(first, SPAN)], ones_b[:, :], onehot[s][:, i, :],
                                            start=False, stop=True, skip_group_check=True)
                    ins.then_inc(sums_done[l], 1)

                def products(g, s):
                    pe.wait_ge(win_copied[l], g + 1)
                    if not (known(g) and g < 1):
                        pe.wait_ge(evacuated[l], g * EV[l])
                    for b in range(r):
                        ins = pe.matmul(prod_ps[:, 0:WINDOW], weights[l][:, b, :],
                                        win_sb[s][:, b * WINDOW:(b + 1) * WINDOW], start=b == 0, stop=b == r - 1)
                    ins.then_inc(prod_done[l], 1)

                def fast():
                    if l:
                        spread_types(0, 0, 0)
                        sum_coef(0)
                        spread_types(1, 1, 0)

                    def step(g, s, k):
                        if l and not (known(g) and g == groups - 1):
                            pe.wait_ge(hots_ready[l], 2 * g + 1)
                            sum_coef(g + 1)
                        sums(g, s, k)
                        if l and not (known(g) and g >= groups - 2):
                            spread_types(g + 2, s, k + 1)
                        if not (known(g) and g == 0):
                            products(g - 1, 1 - s)
                    over_groups(pe, step)
                    products(groups - 1, 1)

                def general_path():
                    pe.sem_inc(g_sums[l], 1)
                    with pe.Fori(0, pairs) as k:
                        for s in range(2):
                            g = 2 * k + s
                            if l:
                                pe.wait_ge(g_added[l], g * (2 * GROUP) + 1)
                                pe.wait_ge(type_row_in[s], (k + 1) * 16)
                                spread_types(g, s, k)
                                sum_coef(g)
                            with pe.Fori(0, GROUP) as i:
                                for h in range(2):
                                    u = (g * GROUP + i) * 2 + h
                                    pe.wait_ge(g_rows[l], g * GROUP + i + 1)
                                    pe.wait_ge(g_sel[l], u + 1)
                                    for b in range(HALF * r // BANK):
                                        ins = pe.matmul(win_ps[0][:, b * BANK:(b + 1) * BANK], one_chunk[:, :],
                                                        sel[0][:, b * BANK:(b + 1) * BANK], start=True, stop=True)
                                    ins.then_inc(g_sums[l], 1)
                                    pe.wait_ge(g_copied[l], u + 1)
                                    pe.wait_ge(g_added[l], u + 1)
                                    for b in range(r):
                                        ins = pe.matmul(prod_ps[:, 0:HALF], weights[l][:, b, :],
                                                        win_sb[0][:, b * HALF:(b + 1) * HALF],
                                                        start=b == 0, stop=b == r - 1)
                                    ins.then_inc(g_prod[l], 1)

                paths(pe, fast, general_path)

                def node_step_tensor(b, s, k, n):
                    pe.wait_ge(x_in_landed[l][s], (k + 1) * 16)
                    for j, m in parts_of(n):
                        ins = pe.transpose(win_ps[s][:, j * P:j * P + m], x_in[s][0:m, j, :], ident[0:m, 0:m])
                    ins.then_inc(x_turned[l], 1)
                    pe.wait_ge(x_t_copied[l], b + 1)
                    if l == 0:
                        pe.wait_ge(mean_step[l], 3 * b + 3)
                    pe.matmul(win_ps[s][:, BANK:BANK + n], w_node[l][:, :], x_t[:, 0:n], start=True, stop=False)
                    pe.matmul(win_ps[s][:, BANK:BANK + n], ident[:, :], agg[:, span_of(b, n)],
                              start=False, stop=True).then_inc(node_summed[l], 1)
                    pe.wait_ge(act_ready[l], b + 1)
                    if not (known(b) and b < 2):
                        pe.wait_ge(moments_ready[l], b - 1)
                    for j, m in parts_of(n):
                        ins = pe.transpose(deg_ps[s][0:m, j * P:(j + 1) * P], act_t[:, j * P:j * P + m], ident[:, :])
                    ins.then_inc(act_turned[l], 1)
                pe.wait_ge(stream_done[l], 1)
                over_batches(pe, node_step_tensor)

        @block.vector
        def _(v):
            count = 0

            def done(ins):
                nonlocal count
                count += 1
                ins.then_inc(prep, 1)
                v.wait_ge(prep, count)

            def over_edges(a):
                return a[:, :].unsqueeze(2).to_broadcast([P, tiles, P])

            v.memset(ones_b[:, :], 1.0)
            v.memset(eps[:, :], EPS)
            done(v.memset(zeros_b[:, :], 0.0))
            v.wait_ge(consts_set, 2)
            v.tensor_copy(iota_f[:, :], iota_i[:, :])
            done(v.tensor_copy(lane_f[:, :], lane_i[:, :]))
            v.tensor_scalar(ident[:, :], iota_f[:, :], lane_f[:, 0:1], None, ALU.is_equal).then_inc(ident_ready, 1)
            v.wait_ge(src_in, 48)
            v.tensor_copy(src_f[:, :, :], src_nat[:, :, :]).then_inc(src_float, 1)
            v.wait_ge(dst_in, 48)
            done(v.tensor_copy(dst_f[:, :, :], dst_nat[:, :, :]))
            done(v.tensor_reduce(low[:, :], dst_f[:, :, :], AX.X, ALU.min))
            done(v.tensor_copy(low_i[:, :], low[:, :]))
            done(v.tensor_scalar(base8_i[:, :], low_i[:, :], 2 * FAR - STEP, None, ALU.bitwise_and))
            done(v.tensor_copy(base8[:, :], base8_i[:, :]))
            no_pads = type_col[:, :].rearrange("p (j e) -> p j e", e=P)
            done(v.scalar_tensor_tensor(out=no_pads, in0=dst_f[:, :, :], scalar=float(FAR), in1=dst_f[:, :, :],
                                        op0=ALU.is_lt, op1=ALU.mult))
            done(v.tensor_reduce(high[:, :], no_pads, AX.X, ALU.max))
            v.tensor_tensor(span[:, :], high[:, :], base8[:, :], ALU.subtract).then_inc(spans_ready, 1)
            v.tensor_tensor(dst_f[:, :, :], dst_f[:, :, :], over_edges(base8), ALU.subtract).then_inc(rel_ready, 1)
            v.wait_ge(type8_in, 48)
            v.wait_ge(turned, -(-tiles // 4))
            v.tensor_copy(src_f[:, :, :], type_nat[:, :, :]).then_inc(types_float, 1)

            v.wait_ge(lin_in, 32)
            done(v.tensor_reduce(group_base[:, :], base_row[:, 0:cols].rearrange("o (g c) -> o g c", c=GROUP),
                                 AX.X, ALU.min))
            done(v.tensor_tensor(base_row[:, 0:cols].rearrange("o (g c) -> o g c", c=GROUP),
                                 base_row[:, 0:cols].rearrange("o (g c) -> o g c", c=GROUP),
                                 group_base[:, :].unsqueeze(2).to_broadcast([1, groups, GROUP]), ALU.subtract))
            done(v.memset(base_row[:, chunks:cols], 0.0))
            v.tensor_copy(offset[:, :], base_row[:, 0:cols]).then_inc(plan_ready, 1)
            v.tensor_copy(group_node[:, :], group_base[:, :]).then_inc(plan_ready, 1)
            v.tensor_reduce(worst[:, 0:1], span_row[:, 0:chunks], AX.X, ALU.max)
            done(v.tensor_reduce(worst[:, 1:2], base_row[:, 0:cols], AX.X, ALU.max))
            v.tensor_scalar(worst[:, 2:3], worst[:, 0:1], float(SPAN), None, ALU.is_ge)
            done(v.tensor_scalar(worst[:, 3:4], worst[:, 1:2], float(WINDOW - SPAN), None, ALU.is_gt))
            v.tensor_tensor(general[:, :], worst[:, 2:3], worst[:, 3:4], ALU.add).then_inc(plan_ready, 1)
            v.wait_ge(cols_copied, 4 * -(-tiles // 4))
            done(v.memset(rel_col[:, chunks:tiles * P], -1.0))
            v.wait_ge(sums_zeroed, 2)
            v.wait_ge(plan_ready, 3)

            def later():
                v.tensor_scalar(src_nat[:, :, :], dst_nat[:, :, :], dump, None, ALU.min).then_inc(dst_clamped, 1)
                v.wait_ge(type64_in, 48)
                v.tensor_copy(src_f[:, :, :].bitcast(BF16)[:, :, 0:P], type_nat[:, :, :]).then_inc(types64_float, 1)
            later()
            v.wait_ge(w_in, 16 * 7)
            done(v.tensor_copy(comp_part[:, 0, :], comp[:, :]))
            done(v.tensor_tensor(comp_left[:, 0, :], comp[:, :], comp_part[:, 0, :], ALU.subtract))
            done(v.tensor_copy(comp_part[:, 1, :], comp_left[:, 0, :]))
            done(v.tensor_tensor(comp_left[:, 1, :], comp_left[:, 0, :], comp_part[:, 1, :], ALU.subtract))
            v.tensor_copy(comp_part[:, 2, :], comp_left[:, 1, :]).then_inc(comp_ready, 1)

            def along_chunks(col, g, n):
                return col[:, bass.ds(g * GROUP, GROUP)].unsqueeze(2).to_broadcast([P, GROUP, n])

            def counting(n):
                return iota_f[:, 0:n].unsqueeze(1).to_broadcast([P, GROUP, n])

            def spot_types(g):
                v.wait_ge(types_spread, g + 1)
                for b in range(2):
                    ins = v.tensor_scalar(type_hot[:, b * BANK:(b + 1) * BANK], deg_ps[b][:, :], lane_f[:, 0:1],
                                          None, ALU.is_equal)
                ins.then_inc(type_hot_ready, 1)

            for l in range(2):
                r = fan[l]
                if l:
                    v.memset(agg[:, :], 0.0).then_inc(agg_zeroed, 1)
                    v.wait_ge(agg_zeroed, 1)

                def make_coef(g, s):
                    if l == 0:
                        return v.tensor_tensor(coef[s][:, :, 0:r], counting(r), along_chunks(type_col, g, r), ALU.is_equal)
                    v.wait_ge(coef_summed, g + 1)
                    return v.tensor_tensor(coef[s][:, :, :],
                                           coef_ps[:, 0:GROUP * r].rearrange("p (c r) -> p c r", r=r),
                                           along_chunks(weight_col, g, r), ALU.mult)

                def select(g, s):
                    if not (known(g) and g < 2):
                        v.wait_ge(sums_done[l], g - 1)
                    make_coef(g, s).then_inc(hots_ready[l], 1)
                    v.tensor_tensor(onehot[s][:, :, :], counting(SPAN), along_chunks(rel_col, g, SPAN),
                                    ALU.is_equal).then_inc(hots_ready[l], 1)
                    v.wait_ge(hots_ready[l], 2 * g + 2)
                    v.tensor_tensor(
                        sel[s][:, 0:GROUP * SPAN * r].rearrange("p (c w r) -> p c w r", w=SPAN, r=r),
                        onehot[s][:, :, :].unsqueeze(3).to_broadcast([P, GROUP, SPAN, r]),
                        coef[s][:, :, 0:r].unsqueeze(2).to_broadcast([P, GROUP, SPAN, r]),
                        ALU.mult).then_inc(sel_ready[l], 1)

                def add(g, s):
                    node = v.value_load(group_node[0:1, bass.ds(g, 1)], min_val=0, max_val=nodes - 1)
                    at = bass.ds(node, WINDOW)
                    v.wait_ge(prod_done[l], g + 1)
                    if not (known(g) and g < 1):
                        v.wait_ge(evacuated[l], g * EV[l])
                    v.tensor_tensor(agg[:, at], agg[:, at], prod_ps[:, 0:WINDOW], ALU.add).then_inc(evacuated[l], 1)
                    if l == 0:
                        v.tensor_tensor(deg[:, at], deg[:, at], deg_ps[s][:, 0:WINDOW], ALU.add
                                        ).then_inc(evacuated[l], 1)

                def fast():
                    if l:
                        spot_types(0)
                    select(0, 0)
                    if l:
                        spot_types(1)

                    def step(g, s, k):
                        if not (known(g) and g == groups - 1):
                            select(g + 1, 1 - s)
                        if l and not (known(g) and g >= groups - 2):
                            spot_types(g + 2)
                        if not (known(g) and g == 0):
                            add(g - 1, 1 - s)
                    over_groups(v, step)
                    add(groups - 1, 1)

                def general_path():
                    v.sem_inc(g_added[l], 1)
                    v.wait_ge(dst_out, 16)
                    with v.Fori(0, groups) as g:
                        if l:
                            spot_types(g)
                        make_coef(g, 0).then_inc(g_coef[l], 1)
                        v.wait_ge(g_coef[l], g + 1)
                        v.sem_inc(vector_paced, 1)
                        with v.Fori(0, GROUP) as i:
                            for h in range(2):
                                u = (g * GROUP + i) * 2 + h
                                v.wait_ge(g_sums[l], u + 1)
                                v.tensor_tensor(
                                    sel[0][:, 0:HALF * r].rearrange("p (w r) -> p w r", r=r),
                                    ident[:, h * HALF:(h + 1) * HALF].unsqueeze(2).to_broadcast([P, HALF, r]),
                                    coef[0][:, bass.ds(i, 1), 0:r].to_broadcast([P, HALF, r]),
                                    ALU.mult).then_inc(g_sel[l], 1)
                                v.wait_ge(g_prod[l], u + 1)
                                v.sem_inc(vector_paced, 1)
                                v.drain()
                                with v.Fori(0, HALF) as w:
                                    node = v.value_load(dst_lin[bass.ds(u * HALF + w, 1)].rearrange("(o e) -> o e", o=1),
                                                        min_val=0, max_val=dump)
                                    at = bass.ds(node, 1)
                                    v.tensor_tensor(agg[:, at], agg[:, at], prod_ps[:, bass.ds(w, 1)], ALU.add)
                                    if l == 0:
                                        v.tensor_scalar(deg[:, at], deg[:, at], 1.0, None, ALU.add)
                                    v.drain()
                                v.sem_inc(g_added[l], 1)

                paths(v, fast, general_path)
                v.drain().then_inc(stream_done[l], 1)
                v.wait_ge(stream_done[l], 1)

                def mean(b, n):
                    at = span_of(b, n)
                    v.tensor_scalar(deg[:, at], deg[:, at], 1.0, None, ALU.max).then_inc(mean_step[l], 1)
                    v.wait_ge(mean_step[l], 3 * b + 1)
                    v.sem_inc(vector_paced, 1)
                    v.reciprocal(deg[:, at], deg[:, at]).then_inc(mean_step[l], 1)
                    v.wait_ge(mean_step[l], 3 * b + 2)
                    v.tensor_tensor(agg[:, at], agg[:, at], deg[:, at], ALU.mult).then_inc(mean_step[l], 1)

                def residual(b, s, n):
                    parts = parts_of(n)
                    m, c = min(n, P), len(parts)
                    v.wait_ge(act_turned[l], b + 1)
                    if not (known(b) and b < 2):
                        v.wait_ge(normed[l], b - 1)
                    v.tensor_tensor(y[s][0:m, 0:c, :], deg_ps[s][0:m, 0:c * P].rearrange("p (c f) -> p c f", f=P),
                                    x_in[s][0:m, 0:c, :], ALU.add).then_inc(node_step[l], 1)
                    v.wait_ge(node_step[l], 2 * b + 1)
                    for j, _ in parts:
                        ins = v.bn_stats(stats[s][0:m, j, :], y[s][0:m, j, :])
                    ins.then_inc(node_step[l], 1)
                    v.wait_ge(node_step[l], 2 * b + 2)
                    v.sem_inc(vector_paced, 1)
                    for j, _ in parts:
                        ins = v.bn_aggr(moments[s][0:m, j, :], stats[s][0:m, j, :])
                    ins.then_inc(moments_ready[l], 1)

                def scale(b, s, n):
                    m, c = min(n, P), len(parts_of(n))
                    v.wait_ge(std_ready[l], b + 1)
                    v.reciprocal(rstd[s][0:m, 0:c], std[s][0:m, 0:c]).then_inc(inverted[l], 1)
                    v.wait_ge(inverted[l], b + 1)
                    v.scalar_tensor_tensor(out=shift[s][0:m, 0:c], in0=moments[s][0:m, 0:c, 0], scalar=-1.0,
                                           in1=rstd[s][0:m, 0:c], op0=ALU.mult, op1=ALU.mult
                                           ).then_inc(rstd_ready[l], 1)

                def node_step_vector(b, s, k, n):
                    if l == 0:
                        mean(b, n)
                    residual(b, s, n)
                    if not (known(b) and b < 1):
                        scale(b - 1, 1 - s, NB)
                    if n != NB:
                        scale(b, s, n)
                over_batches(v, node_step_vector)


_INS = ["x", "src", "dst", "edge_type_64", "edge_type_8", "edge_weight1", "L0_gnn_W_rel", "L0_gnn_W_self_w",
        "L0_gnn_W_self_b", "L1_gnn_weight", "L1_gnn_w_comp", "L1_gnn_h_bias", "L1_gnn_loop_weight"]


def kernel(**inputs):
    import numpy as np
    import concourse.bacc as bacc
    from concourse.bass_utils import run_bass_kernel_spmd

    nc = bacc.Bacc("TRN2", target_bir_lowering=False, num_devices=1)
    arrays = {f"{name}_dram": np.ascontiguousarray(inputs[name]) for name in _INS}
    args = [nc.dram_tensor(n, a.shape, mybir.dt.from_np(a.dtype), kind="ExternalInput").ap()
            for n, a in arrays.items()]
    out = nc.dram_tensor("out_dram", inputs["x"].shape, F32, kind="ExternalOutput").ap()
    two_layer_gnn(nc, *args, out)
    result = run_bass_kernel_spmd(nc, [arrays], core_ids=[0])
    return result.results[0]["out_dram"]
```

```python
from contextlib import ExitStack

import concourse.bass as bass
from concourse import mybir

F32 = mybir.dt.float32
BF16 = mybir.dt.bfloat16
I32 = mybir.dt.int32
U32 = mybir.dt.uint32
ALU = mybir.AluOpType
ACT = mybir.ActivationFunctionType
AX = mybir.AxisListType

P = 128
GROUP = 8
SPAN = 16
STEP = 8
WINDOW = 64
BANK = 512
FAR = 8192
EPS = 1e-5
BATCH = 4


def two_layer_gnn(nc, x, src, dst, type64, type8, weight, w_rel, w_self, b_self,
                  w_basis, w_comp, h_bias, w_loop, out):
    nodes, feat = x.shape
    edges = src.shape[0]
    types0 = w_rel.shape[0]
    types1, bases = w_comp.shape
    assert feat == P and nodes < FAR
    chunks = -(-edges // P)
    groups = -(-chunks // (2 * GROUP)) * 2
    cols = groups * GROUP
    tiles = -(-cols // P)
    full_tiles = edges // (P * P)
    rest_rows = edges // P - full_tiles * P
    rest = edges - (edges // P) * P
    pad_nodes = -(-(nodes + WINDOW) // P) * P
    dump = nodes + WINDOW - 1
    assert full_tiles == tiles - 1 and rest > 0
    GE = GROUP * P
    pairs = groups // 2
    NB = BATCH * P
    full_batches = nodes // NB
    last_nodes = nodes - full_batches * NB
    assert full_batches % 2 == 0 and 0 < last_nodes <= P
    quarters = -(-4 * NB * edges // (nodes * 2 * GE))
    margin = 13
    in_stream = full_batches - 1

    def ready_after(b):
        first = quarters + margin
        return first // 4 + ((quarters * b + first % 4) >> 2)

    assert in_stream % 2 == 1 and ready_after(in_stream - 1) + 2 < pairs

    ctx = ExitStack()
    with ctx:
        def sb(name, shape, dt=F32):
            return ctx.enter_context(nc.sbuf_tensor(name, shape, dt))

        def sem(name):
            return ctx.enter_context(nc.semaphore(name))

        x1 = nc.dram_tensor("x1", (nodes, feat), F32, kind="Internal").ap()
        plan_lin = nc.dram_tensor("plan_lin", (2, tiles * P), F32, kind="Internal").ap()
        dst_lin = nc.dram_tensor("dst_lin", (tiles * P * P,), I32, kind="Internal").ap()
        type_lin = nc.dram_tensor("type_lin", (tiles * P * P,), BF16, kind="Internal").ap()

        src_nat = sb("src_nat", [P, tiles, P], I32)
        dst_nat = sb("dst_nat", [P, tiles, P], I32)
        type_nat = sb("type_nat", [P, tiles, P], I32)
        weight_nat = sb("weight_nat", [P, tiles, P])
        src_f = sb("src_f", [P, tiles, P])
        dst_f = sb("dst_f", [P, tiles, P])
        src_col = sb("src_col", [P, tiles * P])
        rel_col = sb("rel_col", [P, tiles * P])
        type_col = sb("type_col", [P, tiles * P])
        weight_col = sb("weight_col", [P, tiles * P])
        low = sb("low", [P, tiles])
        low_i = sb("low_i", [P, tiles], I32)
        base8_i = sb("base8_i", [P, tiles], I32)
        high = sb("high", [P, tiles])
        base_span = sb("base_span", [P, 2 * tiles])
        base8, span = base_span[:, 0:tiles], base_span[:, tiles:2 * tiles]
        base_span_t = sb("base_span_t", [2 * tiles, P])
        group_base = sb("group_base", [1, groups])
        group_node = sb("group_node", [1, groups], I32)
        offset = sb("offset", [1, cols], I32)
        fall = sb("fall", [1, groups])
        worst = sb("worst", [1, 3])
        checks = sb("checks", [1, 3 + in_stream])
        fails = sb("fails", [1, 1])
        general = sb("general", [1, 1], I32)
        iota_i = sb("iota_i", [P, P], I32)
        lane_i = sb("lane_i", [P, 1], I32)
        iota_f = sb("iota_f", [P, P])
        lane_f = sb("lane_f", [P, 1])
        ident = sb("ident", [P, P])
        ones_b = sb("ones_b", [P, P], BF16)
        zeros_b = sb("zeros_b", [P, BANK], BF16)
        w0 = sb("w0", [P, types0, P])
        w1 = sb("w1", [P, bases, P])
        w_self_nat = sb("w_self_nat", [P, P])
        w_node = [sb("w_self_t", [P, P]), sb("w_loop_sb", [P, P])]
        bias = [sb("bias0", [P, 1]), sb("bias1", [P, 1])]
        comp = sb("comp", [P, bases])
        comp_left = sb("comp_left", [P, 2, bases])
        comp_part = sb("comp_part", [P, 3, bases], BF16)
        index = [sb(f"index{s}", [P, GROUP], U32) for s in range(2)]
        rows = [sb(f"rows{s}", [P, GROUP, P]) for s in range(2)]
        onehot = [sb(f"onehot{s}", [P, GROUP, SPAN], BF16) for s in range(2)]
        coef = [sb(f"coef{s}", [P, GROUP, bases]) for s in range(2)]
        sel = [sb(f"sel{s}", [P, GROUP * SPAN * bases]) for s in range(2)]
        base_row, span_row = [a[0:1, 0:tiles * P] for a in sel]
        type_row = [sb(f"type_row{s}", [1, GE], BF16) for s in range(2)]
        type_hot = sb("type_hot", [P, GE], BF16)
        win_sb = sb("win_sb", [P, bases * 2 * WINDOW])
        one_chunk = sb("one_chunk", [P, P])
        agg = sb("agg", [P, pad_nodes])
        deg = sb("deg", [P, pad_nodes])
        x_in = [sb(f"x_in{s}", [P, BATCH, P]) for s in range(2)]
        x_t = sb("x_t", [P, NB])
        act_t = sb("act_t", [P, NB])
        y = [sb(f"y{s}", [P, BATCH, P]) for s in range(2)]
        stats = [sb(f"stats{s}", [P, BATCH, 6]) for s in range(2)]
        moments = [sb(f"moments{s}", [P, BATCH, 2]) for s in range(2)]
        std = [sb(f"std{s}", [P, BATCH]) for s in range(2)]
        eps = sb("eps", [P, 1])
        rstd = [sb(f"rstd{s}", [P, BATCH]) for s in range(2)]
        shift = [sb(f"shift{s}", [P, BATCH]) for s in range(2)]
        y_out = [sb(f"y_out{s}", [P, BATCH, P]) for s in range(2)]

        bank = [ctx.enter_context(nc.psum_tensor(f"bank{i}", [P, 2 * BANK], F32)) for i in range(2)]
        bank += [ctx.enter_context(nc.psum_tensor(f"bank{i}", [P, BANK], F32)) for i in range(2, 6)]
        win_ps, prod_ps, coef_ps = bank[0:2], bank[2], bank[5]
        deg_ps = bank[3:5]

        def by_layer(name):
            return [sem(f"{name}_{l}") for l in range(2)]

        def by_slot(name):
            return [sem(f"{name}_{s}") for s in range(2)]

        src_in, dst_in, type8_in, type64_in = sem("src_in"), sem("dst_in"), sem("type8_in"), sem("type64_in")
        weight_in, w_in = sem("weight_in"), sem("w_in")
        pads_set, consts_set, sums_zeroed = sem("pads_set"), sem("consts_set"), sem("sums_zeroed")
        prep = sem("prep")
        ident_ready, src_float, spans_ready = sem("ident_ready"), sem("src_float"), sem("spans_ready")
        spans_turned, spans_copied = sem("spans_turned"), sem("spans_copied")
        rel_ready, dst_clamped, types_float = sem("rel_ready"), sem("dst_clamped"), sem("types_float")
        types64_float, comp_ready = sem("types64_float"), sem("comp_ready")
        turned, cols_copied = sem("turned"), sem("cols_copied")
        w_self_turned, w_self_copied = sem("w_self_turned"), sem("w_self_copied")
        lin_out, lin_in, dst_out, type_out = sem("lin_out"), sem("lin_in"), sem("dst_out"), sem("type_out")
        plan_ready, cols_ready = sem("plan_ready"), sem("cols_ready")
        rows_used = by_layer("rows_used")
        idx_staged, hots_ready, sel_ready = by_layer("idx_staged"), by_layer("hots_ready"), by_layer("sel_ready")
        rows_landed = [by_slot(f"rows_landed_{l}") for l in range(2)]
        sums_done, win_copied, prod_done = by_layer("sums_done"), by_layer("win_copied"), by_layer("prod_done")
        added, deg_added, stream_done = by_layer("added"), sem("deg_added"), by_layer("stream_done")
        tensor_paced = sem("tensor_paced")
        pool_paced, scalar_paced, vector_paced = sem("pool_paced"), sem("scalar_paced"), sem("vector_paced")
        type_row_in = by_slot("type_row_in")
        types_spread, type_hot_ready, coef_summed = sem("types_spread"), sem("type_hot_ready"), sem("coef_summed")
        agg_zeroed = sem("agg_zeroed")
        g_coef, g_rows, g_sel, g_sums = by_layer("g_coef"), by_layer("g_rows"), by_layer("g_sel"), by_layer("g_sums")
        g_copied, g_prod, g_added = by_layer("g_copied"), by_layer("g_prod"), by_layer("g_added")
        x_in_landed = [by_slot(f"x_in_landed_{l}") for l in range(2)]
        x_turned, x_t_copied, mean_step = by_layer("x_turned"), by_layer("x_t_copied"), by_layer("mean_step")
        node_summed, act_ready, act_turned = by_layer("node_summed"), by_layer("act_ready"), by_layer("act_turned")
        y_ready, stats_ready = by_layer("y_ready"), by_layer("stats_ready")
        rstd_ready, normed = by_layer("rstd_ready"), by_layer("normed")
        moments_ready, std_ready, inverted = by_layer("moments_ready"), by_layer("std_ready"), by_layer("inverted")
        stored = [by_slot(f"stored_{l}") for l in range(2)]

        block = ctx.enter_context(nc.Block())

        fan = [types0, bases]
        weights = [w0, w1]
        PART = GROUP // 2
        HALF = P // 2

        def known(g):
            return isinstance(g, int)

        def over_groups(eng, step):
            over_pairs(eng, step, 0)
            with eng.Fori(1, pairs - 1) as k:
                over_pairs(eng, step, k)
            over_pairs(eng, step, pairs - 1)

        def over_pairs(eng, step, k):
            for s in range(2):
                step(2 * k + s, s, k)

        def stream(eng, step, phase, begin=None):
            def segment(b, s, j, start):
                end = ready_after(b) + (0 if begin else 1)
                with eng.Fori(start, end) as k:
                    over_pairs(eng, step, k)
                if begin:
                    begin(b, NB)
                    over_pairs(eng, step, end)
                phase(b, s, j, NB)

            over_pairs(eng, step, 0)
            for b in range(2):
                segment(b, b, 0, 1 if b == 0 else ready_after(b - 1) + 1)
            with eng.Fori(1, in_stream // 2) as j:
                for s in range(2):
                    segment(2 * j + s, s, j, ready_after(2 * j + s - 1) + 1)
            b = in_stream - 1
            segment(b, 0, b // 2, ready_after(b - 1) + 1)
            with eng.Fori(ready_after(b) + 1, pairs - 1) as k:
                over_pairs(eng, step, k)
            over_pairs(eng, step, pairs - 1)

        def last_batches(phase):
            phase(in_stream, 1, in_stream // 2, NB)
            phase(full_batches, 0, full_batches // 2, last_nodes)

        def over_batches(eng, phase):
            for s in range(2):
                phase(s, s, 0, NB)
            with eng.Fori(1, full_batches // 2 - 1) as j:
                for s in range(2):
                    phase(2 * j + s, s, j, NB)
            for s in range(2):
                phase(full_batches - 2 + s, s, full_batches // 2 - 1, NB)
            phase(full_batches, 0, full_batches // 2, last_nodes)

        def span_of(b, n):
            return bass.ds(b * NB, n)

        def parts_of(n):
            return [(j, min(P, n - j * P)) for j in range(-(-n // P))]

        def all_stored(eng, l):
            for s in range(2):
                eng.wait_ge(stored[l][s], 16 * (full_batches // 2 + 1 - s))

        def paths(eng, fast, general_path):
            verdict = eng.value_load(general[0:1, 0:1], min_val=0, max_val=2)
            with eng.If(verdict < 1):
                fast()
                eng.nop()
            with eng.Else():
                general_path()
                eng.nop()

        @block.sync
        def _(sp):
            def load_edges(a, nat, landed, pads):
                flat = a if len(a.shape) == 1 else a.rearrange("e o -> (e o)")
                n = full_tiles * P * P
                sp.dma_start(nat[:, 0:full_tiles, :],
                             flat[0:n].rearrange("(j p e) -> p j e", p=P, e=P)).then_inc(landed, 16)
                sp.wait_ge(pads_set, pads)
                sp.dma_start(nat[0:rest_rows, full_tiles, :],
                             flat[n:n + rest_rows * P].rearrange("(p e) -> p e", e=P)).then_inc(landed, 16)
                sp.dma_start(nat[rest_rows:rest_rows + 1, full_tiles, 0:rest],
                             flat[n + rest_rows * P:edges].rearrange("(p e) -> p e", e=rest)).then_inc(landed, 16)

            load_edges(src, src_nat, src_in, 1)
            load_edges(dst, dst_nat, dst_in, 2)
            load_edges(type8, type_nat, type8_in, 3)
            load_edges(weight, weight_nat, weight_in, 4)
            sp.dma_start(w_self_nat[:, :], w_self).then_inc(w_in, 16)
            sp.dma_start(w0[:, :, :], w_rel.rearrange("r i o -> i r o")).then_inc(w_in, 16)
            sp.wait_ge(spans_copied, 1)
            sp.dma_start(plan_lin.rearrange("o (j p) -> (o j) p", p=P), base_span_t[:, :]).then_inc(lin_out, 16)
            sp.wait_ge(lin_out, 16)
            sp.dma_start(base_row, plan_lin[0:1, :]).then_inc(lin_in, 16)
            sp.dma_start(span_row, plan_lin[1:2, :]).then_inc(lin_in, 16)

            sp.dma_start(w1[:, :, :], w_basis.rearrange("r i o -> i r o")).then_inc(w_in, 16)
            sp.dma_start(w_node[1][:, :], w_loop).then_inc(w_in, 16)
            sp.dma_start(bias[0][:, :], b_self.rearrange("(o c) -> o c", c=1)).then_inc(w_in, 16)
            sp.dma_start(bias[1][:, :], h_bias.rearrange("(o c) -> o c", c=1)).then_inc(w_in, 16)
            sp.wait_ge(pads_set, 5)
            sp.dma_start(comp[0:types1, :], w_comp).then_inc(w_in, 16)
            sp.wait_ge(dst_clamped, 1)
            sp.dma_start(dst_lin.rearrange("(j p e) -> p j e", p=P, e=P), src_nat[:, :, :]).then_inc(dst_out, 16)
            sp.wait_ge(types_float, 1)
            load_edges(type64, type_nat, type64_in, 5)
            sp.wait_ge(types64_float, 1)
            sp.dma_start(type_lin.rearrange("(j p e) -> p j e", p=P, e=P),
                         src_f[:, :, :].bitcast(BF16)[:, :, 0:P]).then_inc(type_out, 16)

            def load_types(g, s, k):
                if not (known(g) and g < 2):
                    sp.wait_ge(types_spread, g - 1)
                sp.dma_start(type_row[s][:, :], type_lin[bass.ds(g * GE, GE)].rearrange("(o e) -> o e", o=1)
                             ).then_inc(type_row_in[s], 16)
            sp.wait_ge(type_out, 16)
            over_groups(sp, load_types)
            all_stored(sp, 1)
            sp.wait_ge(dst_out, 16)

        @block.gpsimd
        def _(gp):
            gp.memset(src_nat[:, full_tiles, :], 0).then_inc(pads_set, 1)
            gp.memset(dst_nat[:, full_tiles, :], FAR).then_inc(pads_set, 1)
            gp.memset(type_nat[:, full_tiles, :], types0).then_inc(pads_set, 1)
            gp.memset(weight_nat[:, full_tiles, :], 0.0).then_inc(pads_set, 1)
            gp.memset(comp[:, :], 0.0).then_inc(pads_set, 1)
            gp.iota(iota_i[:, :], pattern=[[1, P]], base=0, channel_multiplier=0).then_inc(consts_set, 1)
            gp.iota(lane_i[:, :], pattern=[[1, 1]], base=0, channel_multiplier=1).then_inc(consts_set, 1)
            gp.memset(agg[:, :], 0.0).then_inc(sums_zeroed, 1)
            gp.memset(deg[:, :], 0.0).then_inc(sums_zeroed, 1)

            for l in range(2):
                table = [x, x1][l]
                if l:
                    all_stored(gp, 0)

                def gather(g, s, k):
                    for i in range(GROUP):
                        if i % PART == 0:
                            gp.wait_ge(idx_staged[l], 2 * g + i // PART + 1)
                            gp.sem_inc(pool_paced, 1)
                        gp.indirect_dma_start(rows[s][:, i, :], None, table,
                                              bass.IndirectOffsetOnAxis(index[s][:, i:i + 1], 0)
                                              ).then_inc(rows_landed[l][s], 16)
                over_groups(gp, gather)

        @block.scalar
        def _(sc):
            def stage(l, g, s, part):
                sc.copy(index[s][:, part * PART:(part + 1) * PART],
                        src_col[:, bass.ds(g * GROUP + part * PART, PART)]).then_inc(idx_staged[l], 1)

            def load_x(l, b, s, n):
                source = [x, x1][l]
                if n == NB:
                    sc.dma_start(x_in[s][:, :, :],
                                 source[span_of(b, n), :].rearrange("(j p) f -> p j f", p=P)
                                 ).then_inc(x_in_landed[l][s], 16)
                else:
                    sc.dma_start(x_in[s][0:n, 0, :], source[span_of(b, n), :]).then_inc(x_in_landed[l][s], 16)

            n = 0
            for col in (src_col, rel_col, type_col, weight_col):
                for j in range(0, tiles, 4):
                    w = min(4, tiles - j) * P
                    n += 1
                    sc.wait_ge(turned, n)
                    sc.copy(col[:, j * P:j * P + w], deg_ps[n % 2][:, 0:w]).then_inc(cols_copied, 1)
                    if n == -(-tiles // 4):
                        sc.wait_ge(spans_turned, 1)
                        sc.copy(base_span_t[:, :], coef_ps[0:2 * tiles, 0:P]).then_inc(spans_copied, 1)
                    if n == 1:
                        sc.wait_ge(cols_copied, 1)
                        for part in range(4):
                            stage(0, part // 2, part // 2, part % 2)
            sc.wait_ge(w_self_turned, 1)
            sc.copy(w_node[0][:, :], coef_ps[:, 0:P]).then_inc(w_self_copied, 1)
            sc.wait_ge(cols_copied, n)
            sc.wait_ge(plan_ready, 3)

            for l in range(2):
                r = fan[l]

                if l:
                    all_stored(sc, 0)
                    for part in range(4):
                        stage(l, part // 2, part // 2, part % 2)
                for b in range(2):
                    load_x(l, b, b, NB)

                def fast():
                    def step(g, s, k):
                        more = not (known(g) and g >= groups - 2)
                        if more:
                            sc.wait_ge(rows_used[l], g + 1)
                            sc.sem_inc(scalar_paced, 1)
                            stage(l, g + 2, s, 0)
                        sc.wait_ge(sums_done[l], g + 1)
                        if more:
                            sc.sem_inc(scalar_paced, 1)
                            stage(l, g + 2, s, 1)
                        if s == 0 and not (known(k) and k == 0):
                            sc.wait_ge(prod_done[l], k)
                        sc.copy(win_sb[:, 0:2 * WINDOW * r].rearrange("p (r s w) -> p r s w", r=r, s=2)[:, :, s, :],
                                win_ps[s][:, 0:WINDOW * r].rearrange("p (w r) -> p r w", r=r)
                                ).then_inc(win_copied[l], 1)
                    stream(sc, step, node_phase)
                    last_batches(node_phase)

                def general_path():
                    with sc.Fori(0, pairs) as k:
                        for s in range(2):
                            g = 2 * k + s
                            sc.wait_ge(rows_landed[l][s], (k + 1) * (16 * GROUP))
                            sc.sem_inc(scalar_paced, 1)
                            with sc.Fori(0, GROUP) as i:
                                for h in range(2):
                                    u = (g * GROUP + i) * 2 + h
                                    if h == 0:
                                        sc.wait_ge(g_sums[l], u + 1)
                                        sc.sem_inc(scalar_paced, 1)
                                        sc.copy(one_chunk[:, :], rows[s][:, bass.ds(i, 1), :].rearrange(
                                            "p o f -> p (o f)")).then_inc(g_rows[l], 1)
                                    sc.wait_ge(g_sums[l], u + 2)
                                    sc.copy(win_sb[:, 0:HALF * r].rearrange("p (r w) -> p r w", r=r),
                                            win_ps[0][:, 0:HALF * r].rearrange("p (w r) -> p r w", r=r)
                                            ).then_inc(g_copied[l], 1)
                            for part in range(2):
                                stage(l, g + 2, s, part)
                    sc.wait_ge(stream_done[l], 1)
                    over_batches(sc, node_phase)

                def finish(b, s, k, n):
                    sc.wait_ge(rstd_ready[l], b + 1)
                    if not (known(b) and b < 2):
                        sc.wait_ge(stored[l][s], k * 16)
                    for j, m in parts_of(n):
                        ins = sc.activation(y_out[s][0:m, j, :], y[s][0:m, j, :], ACT.Identity,
                                            bias=shift[s][0:m, j:j + 1], scale=rstd[s][0:m, j:j + 1])
                    ins.then_inc(normed[l], 1)
                    target = [x1, out][l]
                    sc.wait_ge(normed[l], b + 1)
                    if n == NB:
                        sc.dma_start(target[span_of(b, n), :].rearrange("(j p) f -> p j f", p=P),
                                     y_out[s][:, :, :]).then_inc(stored[l][s], 16)
                    else:
                        sc.dma_start(target[span_of(b, n), :], y_out[s][0:n, 0, :]).then_inc(stored[l][s], 16)

                def deviation(b, s, n):
                    sc.wait_ge(moments_ready[l], b + 1)
                    m, c = min(n, P), len(parts_of(n))
                    sc.activation(std[s][0:m, 0:c], moments[s][0:m, 0:c, 1], ACT.Sqrt,
                                  bias=eps[0:m, 0:1]).then_inc(std_ready[l], 1)

                def node_phase(b, s, k, n):
                    if not (known(b) and b == 0):
                        deviation(b - 1, 1 - s, NB)
                        if n == NB:
                            load_x(l, b + 1, 1 - s, last_nodes if known(b) and b == full_batches - 1 else NB)
                    sc.wait_ge(x_turned[l], b + 1)
                    sc.copy(x_t[:, 0:n], prod_ps[:, 0:n]).then_inc(x_t_copied[l], 1)
                    sc.wait_ge(node_summed[l], b + 1)
                    sc.activation(act_t[:, 0:n], prod_ps[:, 0:n], ACT.Relu,
                                  bias=bias[l][:, 0:1]).then_inc(act_ready[l], 1)
                    if not (known(b) and b == 0):
                        finish(b - 1, 1 - s, k if s else k - 1, NB)
                    if n != NB:
                        deviation(b, s, n)
                        finish(b, s, k, n)

                if l == 0:
                    sc.wait_ge(w_in, 16 * 7)
                paths(sc, fast, general_path)

        @block.tensor
        def _(pe):
            n = 0
            pe.wait_ge(ident_ready, 1)
            for nat, ready, amount in ((src_f, src_float, 1), (dst_f, rel_ready, 1),
                                       (src_f, types_float, 1), (weight_nat, weight_in, 48)):
                pe.wait_ge(ready, amount)
                for j in range(0, tiles, 4):
                    w = min(4, tiles - j)
                    n += 1
                    if n > 2:
                        pe.wait_ge(cols_copied, n - 2)
                    for i in range(w):
                        ins = pe.transpose(deg_ps[n % 2][:, i * P:(i + 1) * P], nat[:, j + i, :], ident[:, :])
                    ins.then_inc(turned, 1)
                if nat is src_f and ready is src_float:
                    pe.wait_ge(spans_ready, 1)
                    pe.transpose(coef_ps[0:2 * tiles, 0:P], base_span[:, :], ident[:, :]).then_inc(spans_turned, 1)
            pe.wait_ge(w_in, 16 * 7)
            pe.wait_ge(spans_copied, 1)
            pe.transpose(coef_ps[:, 0:P], w_self_nat[:, :], ident[:, :]).then_inc(w_self_turned, 1)
            pe.wait_ge(w_self_copied, 1)
            pe.wait_ge(cols_copied, n)
            pe.wait_ge(plan_ready, 3)
            pe.wait_ge(comp_ready, 1)
            shifts = [pe.alloc_register(f"shift{i}") for i in range(GROUP)]

            def spread_types(g, s, k):
                pe.wait_ge(type_row_in[s], (k + 1) * 16)
                for b in range(2):
                    ins = pe.matmul(deg_ps[b][:, :], ones_b[0:1, :], type_row[s][:, b * BANK:(b + 1) * BANK],
                                    start=True, stop=True)
                ins.then_inc(types_spread, 1)

            def sum_coef(g):
                pe.wait_ge(type_hot_ready, g + 1)
                for i in range(GROUP):
                    for part in range(3):
                        ins = pe.matmul(coef_ps[:, i * bases:(i + 1) * bases], type_hot[:, i * P:(i + 1) * P],
                                        comp_part[:, part, :], start=part == 0, stop=part == 2)
                ins.then_inc(coef_summed, 1)

            for l in range(2):
                r = fan[l]

                def sums(g, s, k):
                    if not (known(g) and g < 2):
                        pe.wait_ge(win_copied[l], g - 1)
                    for b in range(WINDOW * r // BANK):
                        pe.matmul(win_ps[s][:, b * BANK:(b + 1) * BANK], zeros_b[:, 0:P], zeros_b[:, :],
                                  start=True, stop=False, skip_group_check=True)
                    pe.load(shifts, offset[0:1, bass.ds(g * GROUP, GROUP)])
                    pe.wait_ge(sel_ready[l], g + 1)
                    pe.wait_ge(rows_landed[l][s], (k + 1) * (16 * GROUP))
                    firsts = [pe.snap(a, min_val=0, max_val=WINDOW - SPAN) for a in shifts]
                    for i in range(GROUP):
                        for h in range(SPAN * r // P):
                            ins = pe.matmul(win_ps[s][:, bass.ds(firsts[i] * r + h * P, P)], rows[s][:, i, :],
                                            sel[s][:, i * SPAN * r + h * P:i * SPAN * r + (h + 1) * P],
                                            start=False, stop=True, skip_group_check=True)
                        if i == PART - 1:
                            ins.then_inc(rows_used[l], 1)
                    if l == 0:
                        if not (known(g) and g < 2):
                            pe.wait_ge(deg_added, g - 1)
                        pe.matmul(deg_ps[s][:, 0:WINDOW], ones_b[:, :], zeros_b[:, 0:WINDOW],
                                  start=True, stop=False, skip_group_check=True)
                        for i in range(GROUP):
                            ins = pe.matmul(deg_ps[s][:, bass.ds(firsts[i], SPAN)], ones_b[:, :], onehot[s][:, i, :],
                                            start=False, stop=True, skip_group_check=True)
                    return ins

                def products(k):
                    pe.wait_ge(win_copied[l], 2 * k + 2)
                    if not (known(k) and k == 0):
                        pe.wait_ge(added[l], 2 * k)
                    for b in range(r):
                        ins = pe.matmul(prod_ps[:, 0:2 * WINDOW], weights[l][:, b, :],
                                        win_sb[:, b * 2 * WINDOW:(b + 1) * 2 * WINDOW], start=b == 0, stop=b == r - 1)
                    ins.then_inc(prod_done[l], 1)

                def fast():
                    if l:
                        spread_types(0, 0, 0)
                        sum_coef(0)
                        spread_types(1, 1, 0)

                    def step(g, s, k):
                        if l and not (known(g) and g == groups - 1):
                            pe.wait_ge(hots_ready[l], 2 * g + 1)
                            sum_coef(g + 1)
                        done = sums(g, s, k)
                        done.then_inc(sums_done[l], 1)
                        if l and not (known(g) and g >= groups - 2):
                            spread_types(g + 2, s, k + 1)
                        if s == 0 and not (known(k) and k == 0):
                            products(k - 1)
                    stream(pe, step, lambda b, s, k, n: node_phase(b, s, k, n, 2 * (ready_after(b) + 1) - 2))
                    products(pairs - 1)
                    last_batches(lambda b, s, k, n: node_phase(b, s, k, n, groups))

                def general_path():
                    pe.sem_inc(g_sums[l], 1)
                    with pe.Fori(0, pairs) as k:
                        for s in range(2):
                            g = 2 * k + s
                            if l:
                                pe.wait_ge(g_added[l], g * (2 * GROUP) + 1)
                                pe.wait_ge(type_row_in[s], (k + 1) * 16)
                                spread_types(g, s, k)
                                sum_coef(g)
                            with pe.Fori(0, GROUP) as i:
                                for h in range(2):
                                    u = (g * GROUP + i) * 2 + h
                                    pe.wait_ge(g_rows[l], g * GROUP + i + 1)
                                    pe.wait_ge(g_sel[l], u + 1)
                                    for b in range(HALF * r // BANK):
                                        ins = pe.matmul(win_ps[0][:, b * BANK:(b + 1) * BANK], one_chunk[:, :],
                                                        sel[0][:, b * BANK:(b + 1) * BANK], start=True, stop=True)
                                    ins.then_inc(g_sums[l], 1)
                                    pe.wait_ge(g_copied[l], u + 1)
                                    pe.wait_ge(g_added[l], u + 1)
                                    for b in range(r):
                                        ins = pe.matmul(prod_ps[:, 0:HALF], weights[l][:, b, :],
                                                        win_sb[:, b * HALF:(b + 1) * HALF],
                                                        start=b == 0, stop=b == r - 1)
                                    ins.then_inc(g_prod[l], 1)

                    over_batches(pe, lambda b, s, k, n: node_phase(b, s, k, n, None))

                def node_phase(b, s, k, n, groups_added):
                    if groups_added is None:
                        pe.wait_ge(stream_done[l], 1)
                    else:
                        pe.wait_ge(added[l], groups_added)
                    pe.wait_ge(x_in_landed[l][s], (k + 1) * 16)
                    for j, m in parts_of(n):
                        ins = pe.transpose(prod_ps[:, j * P:j * P + m], x_in[s][0:m, j, :], ident[0:m, 0:m])
                    ins.then_inc(x_turned[l], 1)
                    pe.wait_ge(x_t_copied[l], b + 1)
                    pe.matmul(prod_ps[:, 0:n], w_node[l][:, :], x_t[:, 0:n], start=True, stop=False)
                    if l == 0:
                        pe.wait_ge(mean_step[l], 3 * b + 3)
                    pe.matmul(prod_ps[:, 0:n], ident[:, :], agg[:, span_of(b, n)],
                              start=False, stop=True).then_inc(node_summed[l], 1)
                    pe.wait_ge(act_ready[l], b + 1)
                    for j, m in parts_of(n):
                        ins = pe.transpose(prod_ps[0:m, j * P:(j + 1) * P], act_t[:, j * P:j * P + m], ident[:, :])
                    ins.then_inc(act_turned[l], 1)
                    pe.wait_ge(y_ready[l], b + 1)
                    pe.sem_inc(tensor_paced, 1)

                paths(pe, fast, general_path)

        @block.vector
        def _(v):
            count = 0

            def done(ins):
                nonlocal count
                count += 1
                ins.then_inc(prep, 1)
                v.wait_ge(prep, count)

            def over_edges(a):
                return a[:, :].unsqueeze(2).to_broadcast([P, tiles, P])

            v.memset(ones_b[:, :], 1.0)
            v.memset(eps[:, :], EPS)
            done(v.memset(zeros_b[:, :], 0.0))
            v.wait_ge(consts_set, 2)
            v.tensor_copy(iota_f[:, :], iota_i[:, :])
            done(v.tensor_copy(lane_f[:, :], lane_i[:, :]))
            v.tensor_scalar(ident[:, :], iota_f[:, :], lane_f[:, 0:1], None, ALU.is_equal).then_inc(ident_ready, 1)
            v.wait_ge(src_in, 48)
            v.tensor_copy(src_f[:, :, :], src_nat[:, :, :]).then_inc(src_float, 1)
            v.wait_ge(dst_in, 48)
            done(v.tensor_copy(dst_f[:, :, :], dst_nat[:, :, :]))
            done(v.tensor_reduce(low[:, :], dst_f[:, :, :], AX.X, ALU.min))
            done(v.tensor_copy(low_i[:, :], low[:, :]))
            done(v.tensor_scalar(base8_i[:, :], low_i[:, :], 2 * FAR - STEP, None, ALU.bitwise_and))
            done(v.tensor_copy(base8[:, :], base8_i[:, :]))
            no_pads = type_col[:, :].rearrange("p (j e) -> p j e", e=P)
            done(v.scalar_tensor_tensor(out=no_pads, in0=dst_f[:, :, :], scalar=float(FAR), in1=dst_f[:, :, :],
                                        op0=ALU.is_lt, op1=ALU.mult))
            done(v.tensor_reduce(high[:, :], no_pads, AX.X, ALU.max))
            v.tensor_tensor(span[:, :], high[:, :], base8[:, :], ALU.subtract).then_inc(spans_ready, 1)
            v.tensor_tensor(dst_f[:, :, :], dst_f[:, :, :], over_edges(base8), ALU.subtract).then_inc(rel_ready, 1)
            v.wait_ge(type8_in, 48)
            v.wait_ge(turned, -(-tiles // 4))
            v.tensor_copy(src_f[:, :, :], type_nat[:, :, :]).then_inc(types_float, 1)

            v.wait_ge(lin_in, 32)
            done(v.tensor_reduce(group_base[:, :], base_row[:, 0:cols].rearrange("o (g c) -> o g c", c=GROUP),
                                 AX.X, ALU.min))
            done(v.tensor_tensor(base_row[:, 0:cols].rearrange("o (g c) -> o g c", c=GROUP),
                                 base_row[:, 0:cols].rearrange("o (g c) -> o g c", c=GROUP),
                                 group_base[:, :].unsqueeze(2).to_broadcast([1, groups, GROUP]), ALU.subtract))
            done(v.memset(base_row[:, chunks:cols], 0.0))
            v.tensor_copy(offset[:, :], base_row[:, 0:cols]).then_inc(plan_ready, 1)
            v.tensor_copy(group_node[:, :], group_base[:, :]).then_inc(plan_ready, 1)
            done(v.tensor_tensor(fall[:, 0:groups - 1], group_base[:, 0:groups - 1], group_base[:, 1:groups],
                                 ALU.subtract))
            v.tensor_reduce(worst[:, 2:3], fall[:, 0:groups - 1], AX.X, ALU.max)
            v.tensor_reduce(worst[:, 0:1], span_row[:, 0:chunks], AX.X, ALU.max)
            done(v.tensor_reduce(worst[:, 1:2], base_row[:, 0:cols], AX.X, ALU.max))
            v.tensor_scalar(checks[:, 0:1], worst[:, 0:1], float(SPAN), None, ALU.is_ge)
            v.tensor_scalar(checks[:, 1:2], worst[:, 1:2], float(WINDOW - SPAN), None, ALU.is_gt)
            ins = v.tensor_scalar(checks[:, 2:3], worst[:, 2:3], 0.0, None, ALU.is_gt)
            for b in range(in_stream):
                g = 2 * ready_after(b) - 2
                ins = v.tensor_scalar(checks[:, 3 + b:4 + b], group_base[:, g:g + 1], float(NB * (b + 1)), None,
                                      ALU.is_lt)
            done(ins)
            done(v.tensor_reduce(fails[:, :], checks[:, :], AX.X, ALU.max))
            v.tensor_copy(general[:, :], fails[:, :]).then_inc(plan_ready, 1)
            v.wait_ge(cols_copied, 4 * -(-tiles // 4))
            done(v.memset(rel_col[:, chunks:tiles * P], -1.0))
            v.wait_ge(sums_zeroed, 2)
            v.wait_ge(plan_ready, 3)

            def later():
                v.tensor_scalar(src_nat[:, :, :], dst_nat[:, :, :], dump, None, ALU.min).then_inc(dst_clamped, 1)
                v.wait_ge(type64_in, 48)
                v.tensor_copy(src_f[:, :, :].bitcast(BF16)[:, :, 0:P], type_nat[:, :, :]).then_inc(types64_float, 1)
            later()
            v.wait_ge(w_in, 16 * 7)
            done(v.tensor_copy(comp_part[:, 0, :], comp[:, :]))
            done(v.tensor_tensor(comp_left[:, 0, :], comp[:, :], comp_part[:, 0, :], ALU.subtract))
            done(v.tensor_copy(comp_part[:, 1, :], comp_left[:, 0, :]))
            done(v.tensor_tensor(comp_left[:, 1, :], comp_left[:, 0, :], comp_part[:, 1, :], ALU.subtract))
            v.tensor_copy(comp_part[:, 2, :], comp_left[:, 1, :]).then_inc(comp_ready, 1)

            def along_chunks(col, g, n):
                return col[:, bass.ds(g * GROUP, GROUP)].unsqueeze(2).to_broadcast([P, GROUP, n])

            def counting(n):
                return iota_f[:, 0:n].unsqueeze(1).to_broadcast([P, GROUP, n])

            def spot_types(g):
                v.wait_ge(types_spread, g + 1)
                for b in range(2):
                    ins = v.tensor_scalar(type_hot[:, b * BANK:(b + 1) * BANK], deg_ps[b][:, :], lane_f[:, 0:1],
                                          None, ALU.is_equal)
                ins.then_inc(type_hot_ready, 1)

            for l in range(2):
                r = fan[l]
                if l:
                    v.memset(agg[:, :], 0.0).then_inc(agg_zeroed, 1)
                    v.wait_ge(agg_zeroed, 1)

                def make_coef(g, s):
                    if l == 0:
                        return v.tensor_tensor(coef[s][:, :, 0:r], counting(r), along_chunks(type_col, g, r), ALU.is_equal)
                    v.wait_ge(coef_summed, g + 1)
                    return v.tensor_tensor(coef[s][:, :, :],
                                           coef_ps[:, 0:GROUP * r].rearrange("p (c r) -> p c r", r=r),
                                           along_chunks(weight_col, g, r), ALU.mult)

                def select(g, s):
                    if not (known(g) and g < 2):
                        v.wait_ge(sums_done[l], g - 1)
                    make_coef(g, s).then_inc(hots_ready[l], 1)
                    v.tensor_tensor(onehot[s][:, :, :], counting(SPAN), along_chunks(rel_col, g, SPAN),
                                    ALU.is_equal).then_inc(hots_ready[l], 1)
                    v.wait_ge(hots_ready[l], 2 * g + 2)
                    v.tensor_tensor(
                        sel[s][:, 0:GROUP * SPAN * r].rearrange("p (c w r) -> p c w r", w=SPAN, r=r),
                        onehot[s][:, :, :].unsqueeze(3).to_broadcast([P, GROUP, SPAN, r]),
                        coef[s][:, :, 0:r].unsqueeze(2).to_broadcast([P, GROUP, SPAN, r]),
                        ALU.mult).then_inc(sel_ready[l], 1)

                def add(g, s, k):
                    node = v.value_load(group_node[0:1, bass.ds(g, 1)], min_val=0, max_val=nodes - 1)
                    at = bass.ds(node, WINDOW)
                    v.wait_ge(prod_done[l], k + 1)
                    if not (known(g) and g < 1):
                        v.wait_ge(added[l], g)
                    v.tensor_tensor(agg[:, at], agg[:, at], prod_ps[:, s * WINDOW:(s + 1) * WINDOW], ALU.add
                                    ).then_inc(added[l], 1)

                def add_deg(g, s):
                    node = v.value_load(group_node[0:1, bass.ds(g, 1)], min_val=0, max_val=nodes - 1)
                    at = bass.ds(node, WINDOW)
                    v.wait_ge(sums_done[l], g + 1)
                    if not (known(g) and g < 1):
                        v.wait_ge(deg_added, g)
                    v.tensor_tensor(deg[:, at], deg[:, at], deg_ps[s][:, 0:WINDOW], ALU.add).then_inc(deg_added, 1)

                def fast():
                    if l:
                        spot_types(0)
                    select(0, 0)
                    if l:
                        spot_types(1)

                    def step(g, s, k):
                        if not (known(g) and g == groups - 1):
                            select(g + 1, 1 - s)
                        if l and not (known(g) and g >= groups - 2):
                            spot_types(g + 2)
                        if l == 0 and not (known(g) and g == 0):
                            add_deg(g - 1, 1 - s)
                        if s == 0 and not (known(k) and k == 0):
                            for h in range(2):
                                add(2 * (k - 1) + h, h, k - 1)

                    def mean_of(b, n):
                        if l == 0:
                            mean(b, n, 2 * ready_after(b) - 2)
                    stream(v, step, node_phase, mean_of)
                    if l == 0:
                        add_deg(groups - 1, 1)
                    for h in range(2):
                        add(groups - 2 + h, h, pairs - 1)
                    if l == 0:
                        mean(in_stream, NB, groups)
                    node_phase(in_stream, 1, in_stream // 2, NB)
                    if l == 0:
                        mean(full_batches, last_nodes, groups)
                    node_phase(full_batches, 0, full_batches // 2, last_nodes)

                def general_path():
                    v.sem_inc(g_added[l], 1)
                    v.wait_ge(dst_out, 16)
                    with v.Fori(0, groups) as g:
                        if l:
                            spot_types(g)
                        make_coef(g, 0).then_inc(g_coef[l], 1)
                        v.wait_ge(g_coef[l], g + 1)
                        v.sem_inc(vector_paced, 1)
                        with v.Fori(0, GROUP) as i:
                            for h in range(2):
                                u = (g * GROUP + i) * 2 + h
                                v.wait_ge(g_sums[l], u + 1)
                                v.tensor_tensor(
                                    sel[0][:, 0:HALF * r].rearrange("p (w r) -> p w r", r=r),
                                    ident[:, h * HALF:(h + 1) * HALF].unsqueeze(2).to_broadcast([P, HALF, r]),
                                    coef[0][:, bass.ds(i, 1), 0:r].to_broadcast([P, HALF, r]),
                                    ALU.mult).then_inc(g_sel[l], 1)
                                v.wait_ge(g_prod[l], u + 1)
                                v.sem_inc(vector_paced, 1)
                                v.drain()
                                with v.Fori(0, HALF) as w:
                                    node = v.value_load(dst_lin[bass.ds(u * HALF + w, 1)].rearrange("(o e) -> o e", o=1),
                                                        min_val=0, max_val=dump)
                                    at = bass.ds(node, 1)
                                    v.tensor_tensor(agg[:, at], agg[:, at], prod_ps[:, bass.ds(w, 1)], ALU.add)
                                    if l == 0:
                                        v.tensor_scalar(deg[:, at], deg[:, at], 1.0, None, ALU.add)
                                    v.drain()
                                v.sem_inc(g_added[l], 1)

                    v.drain().then_inc(stream_done[l], 1)
                    v.wait_ge(stream_done[l], 1)
                    v.sem_inc(vector_paced, 1)

                    def both(b, s, k, n):
                        if l == 0:
                            mean(b, n, None)
                        node_phase(b, s, k, n)
                    over_batches(v, both)

                def mean(b, n, groups_added):
                    at = span_of(b, n)
                    if groups_added is not None:
                        v.wait_ge(added[l], groups_added)
                        v.wait_ge(deg_added, groups_added)
                        v.sem_inc(vector_paced, 1)
                    v.tensor_scalar(deg[:, at], deg[:, at], 1.0, None, ALU.max).then_inc(mean_step[l], 1)
                    v.wait_ge(mean_step[l], 3 * b + 1)
                    v.sem_inc(vector_paced, 1)
                    v.reciprocal(deg[:, at], deg[:, at]).then_inc(mean_step[l], 1)
                    v.wait_ge(mean_step[l], 3 * b + 2)
                    v.tensor_tensor(agg[:, at], agg[:, at], deg[:, at], ALU.mult).then_inc(mean_step[l], 1)

                def residual(b, s, n):
                    parts = parts_of(n)
                    m, c = min(n, P), len(parts)
                    v.wait_ge(act_turned[l], b + 1)
                    if not (known(b) and b < 2):
                        v.wait_ge(normed[l], b - 1)
                    v.tensor_tensor(y[s][0:m, 0:c, :], prod_ps[0:m, 0:c * P].rearrange("p (c f) -> p c f", f=P),
                                    x_in[s][0:m, 0:c, :], ALU.add).then_inc(y_ready[l], 1)
                    v.wait_ge(y_ready[l], b + 1)
                    for j, _ in parts:
                        ins = v.bn_stats(stats[s][0:m, j, :], y[s][0:m, j, :])
                    ins.then_inc(stats_ready[l], 1)
                    v.wait_ge(stats_ready[l], b + 1)
                    v.sem_inc(vector_paced, 1)
                    for j, _ in parts:
                        ins = v.bn_aggr(moments[s][0:m, j, :], stats[s][0:m, j, :])
                    ins.then_inc(moments_ready[l], 1)

                def scale(b, s, n):
                    m, c = min(n, P), len(parts_of(n))
                    v.wait_ge(std_ready[l], b + 1)
                    v.reciprocal(rstd[s][0:m, 0:c], std[s][0:m, 0:c]).then_inc(inverted[l], 1)
                    v.wait_ge(inverted[l], b + 1)
                    v.scalar_tensor_tensor(out=shift[s][0:m, 0:c], in0=moments[s][0:m, 0:c, 0], scalar=-1.0,
                                           in1=rstd[s][0:m, 0:c], op0=ALU.mult, op1=ALU.mult
                                           ).then_inc(rstd_ready[l], 1)

                def node_phase(b, s, k, n):
                    if not (known(b) and b == 0):
                        scale(b - 1, 1 - s, NB)
                    residual(b, s, n)
                    if n != NB:
                        scale(b, s, n)

                paths(v, fast, general_path)


_INS = ["x", "src", "dst", "edge_type_64", "edge_type_8", "edge_weight1", "L0_gnn_W_rel", "L0_gnn_W_self_w",
        "L0_gnn_W_self_b", "L1_gnn_weight", "L1_gnn_w_comp", "L1_gnn_h_bias", "L1_gnn_loop_weight"]


def kernel(**inputs):
    import numpy as np
    import concourse.bacc as bacc
    from concourse.bass_utils import run_bass_kernel_spmd

    nc = bacc.Bacc("TRN2", target_bir_lowering=False, num_devices=1)
    arrays = {f"{name}_dram": np.ascontiguousarray(inputs[name]) for name in _INS}
    args = [nc.dram_tensor(n, a.shape, mybir.dt.from_np(a.dtype), kind="ExternalInput").ap()
            for n, a in arrays.items()]
    out = nc.dram_tensor("out_dram", inputs["x"].shape, F32, kind="ExternalOutput").ap()
    two_layer_gnn(nc, *args, out)
    result = run_bass_kernel_spmd(nc, [arrays], core_ids=[0])
    return result.results[0]["out_dram"]
```

```python
from contextlib import ExitStack

import concourse.bass as bass
from concourse import mybir

F32 = mybir.dt.float32
BF16 = mybir.dt.bfloat16
I32 = mybir.dt.int32
U32 = mybir.dt.uint32
ALU = mybir.AluOpType
ACT = mybir.ActivationFunctionType
AX = mybir.AxisListType

P = 128
GROUP = 8
SPAN = 16
STEP = 8
WINDOW = 64
BANK = 512
FAR = 8192
EPS = 1e-5
BATCH = 4


def two_layer_gnn(nc, x, src, dst, type64, type8, weight, w_rel, w_self, b_self,
                  w_basis, w_comp, h_bias, w_loop, out):
    nodes, feat = x.shape
    edges = src.shape[0]
    types0 = w_rel.shape[0]
    types1, bases = w_comp.shape
    assert feat == P and nodes < FAR
    chunks = -(-edges // P)
    groups = -(-chunks // (2 * GROUP)) * 2
    cols = groups * GROUP
    tiles = -(-cols // P)
    full_tiles = edges // (P * P)
    rest_rows = edges // P - full_tiles * P
    rest = edges - (edges // P) * P
    pad_nodes = -(-(nodes + WINDOW) // P) * P
    dump = nodes + WINDOW - 1
    assert full_tiles == tiles - 1 and rest > 0
    GE = GROUP * P
    pairs = groups // 2
    NB = BATCH * P
    full_batches = nodes // NB
    last_nodes = nodes - full_batches * NB
    assert full_batches % 2 == 0 and 0 < last_nodes <= P
    quarters = -(-4 * NB * edges // (nodes * 2 * GE))
    margin = 13
    in_stream = full_batches - 1

    def ready_after(b):
        first = quarters + margin
        return first // 4 + ((quarters * b + first % 4) >> 2)

    assert in_stream % 2 == 1 and ready_after(in_stream - 1) + 3 < pairs
    last_chunks = chunks - (groups - 1) * GROUP
    assert 0 < last_chunks <= GROUP // 2

    ctx = ExitStack()
    with ctx:
        def sb(name, shape, dt=F32):
            return ctx.enter_context(nc.sbuf_tensor(name, shape, dt))

        def sem(name):
            return ctx.enter_context(nc.semaphore(name))

        x1 = nc.dram_tensor("x1", (nodes, feat), F32, kind="Internal").ap()
        dst_lin = nc.dram_tensor("dst_lin", (tiles * P * P,), I32, kind="Internal").ap()
        type_lin = nc.dram_tensor("type_lin", (tiles * P * P,), BF16, kind="Internal").ap()

        src_nat = sb("src_nat", [P, tiles, P], I32)
        dst_nat = sb("dst_nat", [P, tiles, P], I32)
        type_nat = sb("type_nat", [P, tiles, P], I32)
        weight_nat = sb("weight_nat", [P, tiles, P])
        src_f = sb("src_f", [P, tiles, P])
        last_win = sb("last_win", [P, bases * 2 * WINDOW])
        dst_f = last_win[:, 0:tiles * P].rearrange("p (j e) -> p j e", e=P)
        src_col = sb("src_col", [P, tiles * P])
        rel_col = sb("rel_col", [P, tiles * P])
        type_col = sb("type_col", [P, tiles * P])
        weight_col = sb("weight_col", [P, tiles * P])
        low = sb("low", [P, tiles])
        low_i = sb("low_i", [P, tiles], I32)
        base8_i = sb("base8_i", [P, tiles], I32)
        base8 = sb("base8", [P, tiles])
        span = sb("span", [P, tiles])
        base8_t = sb("base8_t", [tiles, P])
        span_t = sb("span_t", [tiles, P])
        per_tile = P // GROUP
        group_base_t = sb("group_base_t", [tiles, per_tile])
        group_span_t = sb("group_span_t", [tiles, per_tile])
        group_reach_t = sb("group_reach_t", [tiles, per_tile])
        offset_f_t = sb("offset_f_t", [tiles, P])
        offset_t = sb("offset_t", [tiles, P], I32)
        group_rows = sb("group_rows", [1, 3, tiles * per_tile])
        group_base = group_rows[:, 0, 0:groups]
        group_span = group_rows[:, 1, 0:groups]
        group_reach = group_rows[:, 2, 0:groups]
        group_node = sb("group_node", [1, groups], I32)
        offset = sb("offset", [1, tiles * P], I32)
        fall = sb("fall", [1, groups])
        worst = sb("worst", [1, 3])
        checks = sb("checks", [1, 3 + in_stream])
        fails = sb("fails", [1, 1])
        general = sb("general", [1, 1], I32)
        iota_i = sb("iota_i", [P, P], I32)
        lane_i = sb("lane_i", [P, 1], I32)
        iota_f = sb("iota_f", [P, P])
        lane_f = sb("lane_f", [P, 1])
        ident = sb("ident", [P, P])
        ones_b = sb("ones_b", [P, P], BF16)
        zeros_b = sb("zeros_b", [P, BANK], BF16)
        w0 = sb("w0", [P, types0, P])
        w1 = sb("w1", [P, bases, P])
        w_self_nat = sb("w_self_nat", [P, P])
        w_node = [sb("w_self_t", [P, P]), sb("w_loop_sb", [P, P])]
        bias = [sb("bias0", [P, 1]), sb("bias1", [P, 1])]
        comp = sb("comp", [P, bases])
        comp_left = sb("comp_left", [P, 2, bases])
        comp_part = sb("comp_part", [P, 3, bases], BF16)
        index = [sb(f"index{s}", [P, GROUP], U32) for s in range(2)]
        rows = [sb(f"rows{s}", [P, GROUP, P]) for s in range(2)]
        onehot = [sb(f"onehot{s}", [P, GROUP, SPAN], BF16) for s in range(2)]
        coef = [sb(f"coef{s}", [P, GROUP, bases]) for s in range(2)]
        sel = [sb(f"sel{s}", [P, GROUP * SPAN * bases]) for s in range(2)]
        type_row = [sb(f"type_row{s}", [1, GE], BF16) for s in range(2)]
        type_hot = sb("type_hot", [P, GE], BF16)
        win_sb = sb("win_sb", [P, bases * 2 * WINDOW])
        one_chunk = sb("one_chunk", [P, P])
        agg = sb("agg", [P, pad_nodes])
        deg = sb("deg", [P, pad_nodes])
        x_in = [sb(f"x_in{s}", [P, BATCH, P]) for s in range(2)]
        x_t = sb("x_t", [P, NB + P])
        act_t = sb("act_t", [P, NB + P])
        y = [sb(f"y{s}", [P, BATCH, P]) for s in range(2)]
        stats = [sb(f"stats{s}", [P, BATCH, 6]) for s in range(2)]
        moments = [sb(f"moments{s}", [P, BATCH, 2]) for s in range(2)]
        std = [sb(f"std{s}", [P, BATCH]) for s in range(2)]
        eps = sb("eps", [P, 1])
        rstd = [sb(f"rstd{s}", [P, BATCH]) for s in range(2)]
        shift = [sb(f"shift{s}", [P, BATCH]) for s in range(2)]
        y_out = [sb(f"y_out{s}", [P, BATCH, P]) for s in range(2)]

        bank = [ctx.enter_context(nc.psum_tensor(f"bank{i}", [P, 2 * BANK], F32)) for i in range(2)]
        bank += [ctx.enter_context(nc.psum_tensor(f"bank{i}", [P, BANK], F32)) for i in range(2, 6)]
        win_ps, prod_ps, coef_ps = bank[0:2], bank[2], bank[5]

        def windows_of(k):
            return last_win if known(k) and k == pairs - 1 else win_sb

        def products_of(k):
            return coef_ps if known(k) and k == pairs - 1 else prod_ps
        deg_ps = bank[3:5]

        def by_layer(name):
            return [sem(f"{name}_{l}") for l in range(2)]

        def by_slot(name):
            return [sem(f"{name}_{s}") for s in range(2)]

        src_in, dst_in, type8_in, type64_in = sem("src_in"), sem("dst_in"), sem("type8_in"), sem("type64_in")
        weight_in, w_in = sem("weight_in"), sem("w_in")
        pads_set, consts_set, sums_zeroed = sem("pads_set"), sem("consts_set"), sem("sums_zeroed")
        prep = sem("prep")
        ident_ready, src_float, groups_ready = sem("ident_ready"), sem("src_float"), sem("groups_ready")
        base_ready, base_turned, base_copied = sem("base_ready"), sem("base_turned"), sem("base_copied")
        span_ready, span_turned, span_copied = sem("span_ready"), sem("span_turned"), sem("span_copied")
        rel_ready, dst_clamped, types_float = sem("rel_ready"), sem("dst_clamped"), sem("types_float")
        types64_float, comp_ready = sem("types64_float"), sem("comp_ready")
        comp_step = sem("comp_step")
        turned, cols_copied = sem("turned"), sem("cols_copied")
        w_self_turned, w_self_copied = sem("w_self_turned"), sem("w_self_copied")
        plan_in, dst_out, type_out = sem("plan_in"), sem("dst_out"), sem("type_out")
        plan_ready, cols_ready = sem("plan_ready"), sem("cols_ready")
        rows_used = by_layer("rows_used")
        idx_staged, hots_ready, sel_ready = by_layer("idx_staged"), by_layer("hots_ready"), by_layer("sel_ready")
        rows_landed = [by_slot(f"rows_landed_{l}") for l in range(2)]
        sums_done, win_copied, prod_done = by_layer("sums_done"), by_layer("win_copied"), by_layer("prod_done")
        added, stream_done = by_layer("added"), by_layer("stream_done")
        deg_summed, deg_added = sem("deg_summed"), sem("deg_added")
        tensor_paced = sem("tensor_paced")
        pool_paced, scalar_paced, vector_paced = sem("pool_paced"), sem("scalar_paced"), sem("vector_paced")
        type_row_in = by_slot("type_row_in")
        types_spread, type_hot_ready, coef_summed = sem("types_spread"), sem("type_hot_ready"), sem("coef_summed")
        agg_zeroed = sem("agg_zeroed")
        g_coef, g_rows, g_sel, g_sums = by_layer("g_coef"), by_layer("g_rows"), by_layer("g_sel"), by_layer("g_sums")
        g_copied, g_prod, g_added = by_layer("g_copied"), by_layer("g_prod"), by_layer("g_added")
        x_in_landed = [by_slot(f"x_in_landed_{l}") for l in range(2)]
        x_turned, x_t_copied, mean_step = by_layer("x_turned"), by_layer("x_t_copied"), by_layer("mean_step")
        node_summed, act_ready, act_turned = by_layer("node_summed"), by_layer("act_ready"), by_layer("act_turned")
        y_ready, stats_ready = by_layer("y_ready"), by_layer("stats_ready")
        rstd_ready, normed = by_layer("rstd_ready"), by_layer("normed")
        moments_ready, std_ready, inverted = by_layer("moments_ready"), by_layer("std_ready"), by_layer("inverted")
        stored = [by_slot(f"stored_{l}") for l in range(2)]

        block = ctx.enter_context(nc.Block())

        fan = [types0, bases]
        weights = [w0, w1]
        PART = GROUP // 2
        HALF = P // 2

        def known(g):
            return isinstance(g, int)

        def chunks_of(g):
            return last_chunks if known(g) and g == groups - 1 else GROUP

        def landed(g, k):
            return k * (16 * GROUP) + 16 * chunks_of(g)

        def over_groups(eng, step):
            over_pairs(eng, step, 0)
            with eng.Fori(1, pairs - 1) as k:
                over_pairs(eng, step, k)
            over_pairs(eng, step, pairs - 1)

        def over_pairs(eng, step, k, *within):
            for s in range(2):
                step(2 * k + s, s, k, *within)

        def stream(eng, step, node_parts, before_last, begin=None):
            def segment(b, s, j, start):
                last = ready_after(b)
                with eng.Fori(start, last + (0 if begin else 1)) as k:
                    over_pairs(eng, step, k)
                if begin:
                    begin(b, NB)
                    over_pairs(eng, step, last)
                node_parts[0](b, s, j, NB)
                over_pairs(eng, step, last + 1, [(lambda part=part: part(b, s, j, NB)) for part in node_parts[1:]])

            over_pairs(eng, step, 0)
            for b in range(2):
                segment(b, b, 0, 1 if b == 0 else ready_after(b - 1) + 2)
            with eng.Fori(1, in_stream // 2) as j:
                for s in range(2):
                    segment(2 * j + s, s, j, ready_after(2 * j + s - 1) + 2)
            b = in_stream - 1
            segment(b, 0, b // 2, ready_after(b - 1) + 2)
            with eng.Fori(ready_after(b) + 2, pairs - 1) as k:
                over_pairs(eng, step, k)
            before_last()
            over_pairs(eng, step, pairs - 1)

        last_batches = [(in_stream, 1, in_stream // 2, NB, deg_ps[0], 0),
                        (full_batches, 0, full_batches // 2, last_nodes, deg_ps[1], NB)]

        def in_last(ps):
            return ps is not prod_ps

        def mean_count(b, ps):
            return 3 * in_stream + 3 + b - in_stream if in_last(ps) else 3 * b + 3

        def over_batches(eng, node_parts):
            def phase(*batch):
                for part in node_parts:
                    part(*batch)
            for s in range(2):
                phase(s, s, 0, NB)
            with eng.Fori(1, full_batches // 2 - 1) as j:
                for s in range(2):
                    phase(2 * j + s, s, j, NB)
            for s in range(2):
                phase(full_batches - 2 + s, s, full_batches // 2 - 1, NB)
            phase(full_batches, 0, full_batches // 2, last_nodes)

        def span_of(b, n):
            return bass.ds(b * NB, n)

        def parts_of(n):
            return [(j, min(P, n - j * P)) for j in range(-(-n // P))]

        def all_stored(eng, l):
            for s in range(2):
                eng.wait_ge(stored[l][s], 16 * (full_batches // 2 + 1 - s))

        def paths(eng, fast, general_path):
            verdict = eng.value_load(general[0:1, 0:1], min_val=0, max_val=2)
            with eng.If(verdict < 1):
                fast()
                eng.nop()
            with eng.Else():
                general_path()
                eng.nop()

        def load_edges(eng, a, nat, landed, pads):
            flat = a if len(a.shape) == 1 else a.rearrange("e o -> (e o)")
            n = full_tiles * P * P
            eng.dma_start(nat[:, 0:full_tiles, :],
                         flat[0:n].rearrange("(j p e) -> p j e", p=P, e=P)).then_inc(landed, 16)
            eng.wait_ge(pads_set, pads)
            eng.dma_start(nat[0:rest_rows, full_tiles, :],
                         flat[n:n + rest_rows * P].rearrange("(p e) -> p e", e=P)).then_inc(landed, 16)
            eng.dma_start(nat[rest_rows:rest_rows + 1, full_tiles, 0:rest],
                         flat[n + rest_rows * P:edges].rearrange("(p e) -> p e", e=rest)).then_inc(landed, 16)

        @block.sync
        def _(sp):
            load_edges(sp, src, src_nat, src_in, 1)
            load_edges(sp, type8, type_nat, type8_in, 3)
            load_edges(sp, weight, weight_nat, weight_in, 4)
            sp.dma_start(w_self_nat[:, :], w_self).then_inc(w_in, 16)
            sp.dma_start(w0[:, :, :], w_rel.rearrange("r i o -> i r o")).then_inc(w_in, 16)
            def row(out, a):
                sp.dma_start(out.rearrange("o (j g) -> o j g", j=tiles), a[:, :]).then_inc(plan_in, 16)
            sp.wait_ge(groups_ready, 1)
            row(group_rows[:, 0, :], group_base_t)
            row(group_rows[:, 2, :], group_reach_t)
            row(offset[:, :], offset_t)
            sp.wait_ge(groups_ready, 2)
            row(group_rows[:, 1, :], group_span_t)

            sp.dma_start(w1[:, :, :], w_basis.rearrange("r i o -> i r o")).then_inc(w_in, 16)
            sp.dma_start(w_node[1][:, :], w_loop).then_inc(w_in, 16)
            sp.dma_start(bias[0][:, :], b_self.rearrange("(o c) -> o c", c=1)).then_inc(w_in, 16)
            sp.dma_start(bias[1][:, :], h_bias.rearrange("(o c) -> o c", c=1)).then_inc(w_in, 16)
            sp.wait_ge(pads_set, 5)
            sp.dma_start(comp[0:types1, :], w_comp).then_inc(w_in, 16)
            sp.wait_ge(types_float, 1)
            load_edges(sp, type64, type_nat, type64_in, 5)
            sp.wait_ge(types64_float, 1)
            sp.dma_start(type_lin.rearrange("(j p e) -> p j e", p=P, e=P),
                         src_f[:, :, :].bitcast(BF16)[:, :, 0:P]).then_inc(type_out, 16)
            sp.wait_ge(dst_clamped, 1)
            sp.dma_start(dst_lin.rearrange("(j p e) -> p j e", p=P, e=P), src_nat[:, :, :]).then_inc(dst_out, 16)

            def load_types(g, s, k):
                if not (known(g) and g < 2):
                    sp.wait_ge(types_spread, g - 1)
                sp.dma_start(type_row[s][:, :], type_lin[bass.ds(g * GE, GE)].rearrange("(o e) -> o e", o=1)
                             ).then_inc(type_row_in[s], 16)
            sp.wait_ge(type_out, 16)
            over_groups(sp, load_types)
            all_stored(sp, 1)
            sp.wait_ge(dst_out, 16)

        @block.gpsimd
        def _(gp):
            gp.memset(src_nat[:, full_tiles, :], 0).then_inc(pads_set, 1)
            gp.memset(dst_nat[:, full_tiles, :], FAR).then_inc(pads_set, 1)
            gp.memset(type_nat[:, full_tiles, :], types0).then_inc(pads_set, 1)
            gp.memset(weight_nat[:, full_tiles, :], 0.0).then_inc(pads_set, 1)
            gp.memset(comp[:, :], 0.0).then_inc(pads_set, 1)
            gp.iota(iota_i[:, :], pattern=[[1, P]], base=0, channel_multiplier=0).then_inc(consts_set, 1)
            gp.iota(lane_i[:, :], pattern=[[1, 1]], base=0, channel_multiplier=1).then_inc(consts_set, 1)
            gp.memset(agg[:, :], 0.0).then_inc(sums_zeroed, 1)
            gp.memset(deg[:, 0:pad_nodes // 2], 0.0).then_inc(sums_zeroed, 1)

            for l in range(2):
                table = [x, x1][l]
                if l:
                    all_stored(gp, 0)

                def gather(g, s, k):
                    for i in range(chunks_of(g)):
                        if i % PART == 0:
                            gp.wait_ge(idx_staged[l], 2 * g + i // PART + 1)
                            gp.sem_inc(pool_paced, 1)
                        gp.indirect_dma_start(rows[s][:, i, :], None, table,
                                              bass.IndirectOffsetOnAxis(index[s][:, i:i + 1], 0)
                                              ).then_inc(rows_landed[l][s], 16)
                over_groups(gp, gather)

        @block.scalar
        def _(sc):
            load_edges(sc, dst, dst_nat, dst_in, 2)

            def stage(l, g, s, part):
                sc.copy(index[s][:, part * PART:(part + 1) * PART],
                        src_col[:, bass.ds(g * GROUP + part * PART, PART)]).then_inc(idx_staged[l], 1)

            def load_x(l, b, s, n):
                source = [x, x1][l]
                if n == NB:
                    sc.dma_start(x_in[s][:, :, :],
                                 source[span_of(b, n), :].rearrange("(j p) f -> p j f", p=P)
                                 ).then_inc(x_in_landed[l][s], 16)
                else:
                    sc.dma_start(x_in[s][0:n, 0, :], source[span_of(b, n), :]).then_inc(x_in_landed[l][s], 16)

            n = 0
            for col in (src_col, rel_col, type_col, weight_col):
                for j in range(0, tiles, 4):
                    w = min(4, tiles - j) * P
                    n += 1
                    sc.wait_ge(turned, n)
                    sc.copy(col[:, j * P:j * P + w], deg_ps[n % 2][:, 0:w]).then_inc(cols_copied, 1)
                    if n == -(-tiles // 4):
                        sc.wait_ge(base_turned, 1)
                        sc.copy(base8_t[:, :], coef_ps[0:tiles, 0:P]).then_inc(base_copied, 1)
                    if n == 2 * -(-tiles // 4):
                        sc.wait_ge(span_turned, 1)
                        sc.copy(span_t[:, :], coef_ps[0:tiles, 0:P]).then_inc(span_copied, 1)
                    if n == 1:
                        sc.wait_ge(cols_copied, 1)
                        for part in range(4):
                            stage(0, part // 2, part // 2, part % 2)
            sc.wait_ge(w_self_turned, 1)
            sc.copy(w_node[0][:, :], coef_ps[:, 0:P]).then_inc(w_self_copied, 1)
            sc.wait_ge(cols_copied, n)
            sc.wait_ge(plan_ready, 2)

            for l in range(2):
                r = fan[l]

                if l:
                    for part in range(4):
                        stage(l, part // 2, part // 2, part % 2)
                    all_stored(sc, 0)
                for b in range(2):
                    load_x(l, b, b, NB)

                def fast():
                    def step(g, s, k, within=None):
                        more = not (known(g) and g >= groups - 2)
                        if more:
                            sc.wait_ge(rows_used[l], g + 1)
                            sc.sem_inc(scalar_paced, 1)
                            stage(l, g + 2, s, 0)
                        sc.wait_ge(sums_done[l], g + 1)
                        if more:
                            sc.sem_inc(scalar_paced, 1)
                            stage(l, g + 2, s, 1)
                        if within:
                            within[s]()
                        if known(k) and k == pairs - 1:
                            copied = [s]
                        elif s == 0:
                            return
                        else:
                            copied = range(2)
                            if not (known(k) and k == 0):
                                sc.wait_ge(prod_done[l], k)
                        windows = windows_of(k)[:, 0:2 * WINDOW * r].rearrange("p (r s w) -> p r s w", r=r, s=2)
                        for h in copied:
                            sc.copy(windows[:, :, h, :],
                                    win_ps[h][:, 0:WINDOW * r].rearrange("p (w r) -> p r w", r=r)
                                    ).then_inc(win_copied[l], 1)
                    def before_last():
                        prepare(*last_batches[0][:4])
                        finish(in_stream - 1, 0, in_stream // 2, NB)
                    stream(sc, step, node_parts, before_last)
                    for b, s, k, n, ps, col in last_batches:
                        copy_x(b, n, ps, col)
                    for batch in last_batches:
                        node_sum(*batch)
                    for b, s, k, n, ps, col in last_batches:
                        deviation(b, s, n)
                    for b, s, k, n, ps, col in last_batches:
                        finish(b, s, k, n)

                def general_path():
                    def pair(k):
                        for s in range(2):
                            g = 2 * k + s
                            sc.wait_ge(rows_landed[l][s], landed(g, k))
                            sc.sem_inc(scalar_paced, 1)
                            with sc.Fori(0, GROUP) as i:
                                for h in range(2):
                                    u = (g * GROUP + i) * 2 + h
                                    if h == 0:
                                        sc.wait_ge(g_sums[l], u + 1)
                                        sc.sem_inc(scalar_paced, 1)
                                        sc.copy(one_chunk[:, :], rows[s][:, bass.ds(i, 1), :].rearrange(
                                            "p o f -> p (o f)")).then_inc(g_rows[l], 1)
                                    sc.wait_ge(g_sums[l], u + 2)
                                    sc.copy(win_sb[:, 0:HALF * r].rearrange("p (r w) -> p r w", r=r),
                                            win_ps[0][:, 0:HALF * r].rearrange("p (w r) -> p r w", r=r)
                                            ).then_inc(g_copied[l], 1)
                            if not known(g):
                                for part in range(2):
                                    stage(l, g + 2, s, part)
                    with sc.Fori(0, pairs - 1) as k:
                        pair(k)
                    pair(pairs - 1)
                    sc.wait_ge(stream_done[l], 1)
                    over_batches(sc, node_parts)

                def finish(b, s, k, n):
                    sc.wait_ge(rstd_ready[l], b + 1)
                    if not (known(b) and b < 2):
                        sc.wait_ge(stored[l][s], k * 16)
                    for j, m in parts_of(n):
                        ins = sc.activation(y_out[s][0:m, j, :], y[s][0:m, j, :], ACT.Identity,
                                            bias=shift[s][0:m, j:j + 1], scale=rstd[s][0:m, j:j + 1])
                    ins.then_inc(normed[l], 1)
                    target = [x1, out][l]
                    sc.wait_ge(normed[l], b + 1)
                    if n == NB:
                        sc.dma_start(target[span_of(b, n), :].rearrange("(j p) f -> p j f", p=P),
                                     y_out[s][:, :, :]).then_inc(stored[l][s], 16)
                    else:
                        sc.dma_start(target[span_of(b, n), :], y_out[s][0:n, 0, :]).then_inc(stored[l][s], 16)

                def deviation(b, s, n):
                    sc.wait_ge(moments_ready[l], b + 1)
                    m, c = min(n, P), len(parts_of(n))
                    sc.activation(std[s][0:m, 0:c], moments[s][0:m, 0:c, 1], ACT.Sqrt,
                                  bias=eps[0:m, 0:1]).then_inc(std_ready[l], 1)

                def prepare(b, s, k, n):
                    if not (known(b) and b == 0):
                        deviation(b - 1, 1 - s, NB)
                        if n == NB:
                            load_x(l, b + 1, 1 - s, last_nodes if known(b) and b == full_batches - 1 else NB)

                def copy_x(b, n, ps=prod_ps, col=0):
                    sc.wait_ge(x_turned[l], b + 1)
                    sc.copy(x_t[:, col:col + n], ps[:, 0:n]).then_inc(x_t_copied[l], 1)

                def node_turn(b, s, k, n):
                    prepare(b, s, k, n)
                    copy_x(b, n)

                def node_sum(b, s, k, n, ps=prod_ps, col=0):
                    sc.wait_ge(node_summed[l], b + 1)
                    sc.activation(act_t[:, col:col + n], ps[:, 0:n], ACT.Relu,
                                  bias=bias[l][:, 0:1]).then_inc(act_ready[l], 1)

                def node_end(b, s, k, n):
                    if not (known(b) and b == 0):
                        finish(b - 1, 1 - s, k if s else k - 1, NB)
                    if n != NB:
                        deviation(b, s, n)
                        finish(b, s, k, n)

                node_parts = (node_turn, node_sum, node_end)

                if l == 0:
                    sc.wait_ge(w_in, 16 * 7)
                paths(sc, fast, general_path)

        @block.tensor
        def _(pe):
            n = 0
            pe.wait_ge(ident_ready, 1)
            for nat, ready, amount in ((src_f, src_float, 1), (dst_f, rel_ready, 1),
                                       (src_f, types_float, 1), (weight_nat, weight_in, 48)):
                pe.wait_ge(ready, amount)
                for j in range(0, tiles, 4):
                    w = min(4, tiles - j)
                    n += 1
                    if n > 2:
                        pe.wait_ge(cols_copied, n - 2)
                    for i in range(w):
                        ins = pe.transpose(deg_ps[n % 2][:, i * P:(i + 1) * P], nat[:, j + i, :], ident[:, :])
                    ins.then_inc(turned, 1)
                if ready is src_float:
                    pe.wait_ge(base_ready, 1)
                    pe.transpose(coef_ps[0:tiles, 0:P], base8[:, :], ident[:, :]).then_inc(base_turned, 1)
                if ready is rel_ready:
                    pe.wait_ge(span_ready, 1)
                    pe.wait_ge(base_copied, 1)
                    pe.transpose(coef_ps[0:tiles, 0:P], span[:, :], ident[:, :]).then_inc(span_turned, 1)
            pe.wait_ge(w_in, 16 * 7)
            pe.wait_ge(span_copied, 1)
            pe.transpose(coef_ps[:, 0:P], w_self_nat[:, :], ident[:, :]).then_inc(w_self_turned, 1)
            pe.wait_ge(w_self_copied, 1)
            pe.wait_ge(cols_copied, n)
            pe.wait_ge(plan_ready, 2)
            shifts = [pe.alloc_register(f"shift{i}") for i in range(GROUP)]

            def spread_types(g, s, k):
                pe.wait_ge(type_row_in[s], (k + 1) * 16)
                for b in range(2):
                    ins = pe.matmul(deg_ps[b][:, :], ones_b[0:1, :], type_row[s][:, b * BANK:(b + 1) * BANK],
                                    start=True, stop=True)
                ins.then_inc(types_spread, 1)

            def sum_coef(g):
                pe.wait_ge(type_hot_ready, g + 1)
                for i in range(GROUP):
                    for part in range(3):
                        ins = pe.matmul(coef_ps[:, i * bases:(i + 1) * bases], type_hot[:, i * P:(i + 1) * P],
                                        comp_part[:, part, :], start=part == 0, stop=part == 2)
                ins.then_inc(coef_summed, 1)

            for l in range(2):
                r = fan[l]

                def load_firsts(g):
                    pe.load(shifts, offset[0:1, bass.ds(g * GROUP, GROUP)])
                    return [pe.snap(a, min_val=0, max_val=WINDOW - SPAN) for a in shifts]

                def deg_sums(g, s, firsts):
                    if not (known(g) and g < 2):
                        pe.wait_ge(deg_added, g - 1)
                    pe.matmul(deg_ps[s][:, 0:WINDOW], ones_b[:, :], zeros_b[:, 0:WINDOW],
                              start=True, stop=False, skip_group_check=True)
                    for i in range(chunks_of(g)):
                        ins = pe.matmul(deg_ps[s][:, bass.ds(firsts[i], SPAN)], ones_b[:, :], onehot[s][:, i, :],
                                        start=False, stop=True, skip_group_check=True)
                    ins.then_inc(deg_summed, 1)

                def sums(g, s, k):
                    if not (known(g) and g < 2):
                        pe.wait_ge(win_copied[l], g - 1)
                    for b in range(WINDOW * r // BANK):
                        pe.matmul(win_ps[s][:, b * BANK:(b + 1) * BANK], zeros_b[:, 0:P], zeros_b[:, :],
                                  start=True, stop=False, skip_group_check=True)
                    firsts = load_firsts(g)
                    pe.wait_ge(sel_ready[l], g + 1)
                    if l == 0 and not (known(g) and g >= groups - 2):
                        deg_sums(g, s, firsts)
                    pe.wait_ge(rows_landed[l][s], landed(g, k))
                    for i in range(chunks_of(g)):
                        for h in range(SPAN * r // P):
                            ins = pe.matmul(win_ps[s][:, bass.ds(firsts[i] * r + h * P, P)], rows[s][:, i, :],
                                            sel[s][:, i * SPAN * r + h * P:i * SPAN * r + (h + 1) * P],
                                            start=False, stop=True, skip_group_check=True)
                        if i == PART - 1 and chunks_of(g) == GROUP:
                            ins.then_inc(rows_used[l], 1)
                    return ins

                def products(k, part):
                    if part == 0:
                        pe.wait_ge(win_copied[l], 2 * k + 2)
                    if part == 0 and not (known(k) and k in (0, pairs - 1)):
                        pe.wait_ge(added[l], 2 * k)
                    for b in range(part * r // 2, (part + 1) * r // 2):
                        ins = pe.matmul(products_of(k)[:, 0:2 * WINDOW], weights[l][:, b, :],
                                        windows_of(k)[:, b * 2 * WINDOW:(b + 1) * 2 * WINDOW],
                                        start=b == 0, stop=b == r - 1)
                    if part:
                        ins.then_inc(prod_done[l], 1)

                if l:
                    pe.wait_ge(comp_ready, 1)

                def fast():
                    if l:
                        spread_types(0, 0, 0)
                        sum_coef(0)
                        spread_types(1, 1, 0)

                    def step(g, s, k, within=None):
                        if l and not (known(g) and g == groups - 1):
                            pe.wait_ge(hots_ready[l], 2 * g + 1)
                            sum_coef(g + 1)
                        done = sums(g, s, k)
                        done.then_inc(sums_done[l], 1)
                        if l and not (known(g) and g >= groups - 2):
                            spread_types(g + 2, s, k + 1)
                        if known(g) and g == groups - 1:
                            if l == 0:
                                pe.wait_ge(deg_added, groups)
                            else:
                                pe.wait_ge(type_hot_ready, groups)
                            for b, slot, turn, n, ps, col in last_batches:
                                turn_x(b, slot, turn, n, ps)
                        if within:
                            within[s]()
                            if s:
                                for part in range(2):
                                    products(k - 1, part)
                        elif not (known(k) and k == 0):
                            products(k - 1, s)
                    def before_last():
                        if l == 0:
                            for s in range(2):
                                firsts = load_firsts(groups - 2 + s)
                                pe.wait_ge(sel_ready[l], groups - 1 + s)
                                deg_sums(groups - 2 + s, s, firsts)
                    stream(pe, step, node_parts(lambda b: 2 * ready_after(b)), before_last)
                    for part in range(2):
                        products(pairs - 1, part)
                    for part in (node_sum, node_end):
                        for batch in last_batches:
                            part(*batch)
                    pe.wait_ge(y_ready[l], full_batches + 1)

                def general_path():
                    pe.sem_inc(g_sums[l], 1)
                    with pe.Fori(0, pairs) as k:
                        for s in range(2):
                            g = 2 * k + s
                            if l:
                                pe.wait_ge(g_added[l], g * (2 * GROUP) + 1)
                                pe.wait_ge(type_row_in[s], (k + 1) * 16)
                                spread_types(g, s, k)
                                sum_coef(g)
                            with pe.Fori(0, GROUP) as i:
                                for h in range(2):
                                    u = (g * GROUP + i) * 2 + h
                                    pe.wait_ge(g_rows[l], g * GROUP + i + 1)
                                    pe.wait_ge(g_sel[l], u + 1)
                                    for b in range(HALF * r // BANK):
                                        ins = pe.matmul(win_ps[0][:, b * BANK:(b + 1) * BANK], one_chunk[:, :],
                                                        sel[0][:, b * BANK:(b + 1) * BANK], start=True, stop=True)
                                    ins.then_inc(g_sums[l], 1)
                                    pe.wait_ge(g_copied[l], u + 1)
                                    pe.wait_ge(g_added[l], u + 1)
                                    for b in range(r):
                                        ins = pe.matmul(prod_ps[:, 0:HALF], weights[l][:, b, :],
                                                        win_sb[:, b * HALF:(b + 1) * HALF],
                                                        start=b == 0, stop=b == r - 1)
                                    ins.then_inc(g_prod[l], 1)

                    over_batches(pe, node_parts(lambda b: None))

                def node_turn(b, s, k, n, groups_added):
                    if groups_added is None:
                        pe.wait_ge(stream_done[l], 1)
                    else:
                        pe.wait_ge(added[l], groups_added)
                    turn_x(b, s, k, n, prod_ps)

                def turn_x(b, s, k, n, ps):
                    pe.wait_ge(x_in_landed[l][s], (k + 1) * 16)
                    for j, m in parts_of(n):
                        ins = pe.transpose(ps[:, j * P:j * P + m], x_in[s][0:m, j, :], ident[0:m, 0:m])
                    ins.then_inc(x_turned[l], 1)

                def node_sum(b, s, k, n, ps=prod_ps, col=0):
                    pe.wait_ge(x_t_copied[l], b + 1)
                    pe.matmul(ps[:, 0:n], w_node[l][:, :], x_t[:, col:col + n], start=True, stop=False)
                    if l == 0:
                        pe.wait_ge(mean_step[l], mean_count(b, ps))
                    elif in_last(ps):
                        pe.wait_ge(added[l], groups)
                    pe.matmul(ps[:, 0:n], ident[:, :], agg[:, span_of(b, n)],
                              start=False, stop=True).then_inc(node_summed[l], 1)

                def node_end(b, s, k, n, ps=prod_ps, col=0):
                    pe.wait_ge(act_ready[l], b + 1)
                    for j, m in parts_of(n):
                        ins = pe.transpose(ps[0:m, j * P:(j + 1) * P], act_t[:, col + j * P:col + j * P + m],
                                           ident[:, :])
                    ins.then_inc(act_turned[l], 1)
                    if not in_last(ps):
                        pe.wait_ge(y_ready[l], b + 1)
                        pe.sem_inc(tensor_paced, 1)

                def node_parts(groups_added):
                    return (lambda b, s, k, n: node_turn(b, s, k, n, groups_added(b))), node_sum, node_end

                paths(pe, fast, general_path)

        @block.vector
        def _(v):
            count = 0

            def done(ins):
                nonlocal count
                count += 1
                ins.then_inc(prep, 1)
                v.wait_ge(prep, count)

            v.memset(ones_b[:, :], 1.0)
            v.memset(eps[:, :], EPS)
            done(v.memset(zeros_b[:, :], 0.0))
            v.wait_ge(consts_set, 2)
            v.tensor_copy(iota_f[:, :], iota_i[:, :])
            done(v.tensor_copy(lane_f[:, :], lane_i[:, :]))
            v.tensor_scalar(ident[:, :], iota_f[:, :], lane_f[:, 0:1], None, ALU.is_equal).then_inc(ident_ready, 1)
            v.memset(deg[:, pad_nodes // 2:], 0.0).then_inc(sums_zeroed, 1)
            v.wait_ge(src_in, 48)
            v.tensor_copy(src_f[:, :, :], src_nat[:, :, :]).then_inc(src_float, 1)
            v.wait_ge(dst_in, 48)
            done(v.tensor_copy(dst_f[:, :, :], dst_nat[:, :, :]))
            done(v.tensor_reduce(low[:, :], dst_f[:, :, :], AX.X, ALU.min))
            done(v.tensor_copy(low_i[:, :], low[:, :]))
            done(v.tensor_scalar(base8_i[:, :], low_i[:, :], 2 * FAR - STEP, None, ALU.bitwise_and))
            v.tensor_copy(base8[:, :], base8_i[:, :]).then_inc(base_ready, 1)
            v.wait_ge(base_ready, 1)
            v.tensor_tensor(dst_f[:, :, :], dst_f[:, :, :], base8[:, :].unsqueeze(2).to_broadcast([P, tiles, P]),
                            ALU.subtract).then_inc(rel_ready, 1)
            v.wait_ge(base_copied, 1)
            by_group = base8_t[:, :].rearrange("j (g c) -> j g c", c=GROUP)
            done(v.tensor_reduce(group_base_t[:, :], by_group, AX.X, ALU.min))
            done(v.tensor_tensor(offset_f_t[:, :].rearrange("j (g c) -> j g c", c=GROUP), by_group,
                                 group_base_t[:, :].unsqueeze(2).to_broadcast([tiles, per_tile, GROUP]),
                                 ALU.subtract))
            done(v.scalar_tensor_tensor(out=offset_f_t[:, :], in0=base8_t[:, :], scalar=float(FAR),
                                        in1=offset_f_t[:, :], op0=ALU.is_lt, op1=ALU.mult))
            v.tensor_copy(offset_t[:, :], offset_f_t[:, :])
            v.tensor_reduce(group_reach_t[:, :], offset_f_t[:, :].rearrange("j (g c) -> j g c", c=GROUP),
                            AX.X, ALU.max).then_inc(groups_ready, 1)
            v.wait_ge(rel_ready, 1)
            v.tensor_reduce(span[:, 0:full_tiles], dst_f[:, 0:full_tiles, :], AX.X, ALU.max)
            no_pads = type_col[:, 0:P]
            done(v.scalar_tensor_tensor(out=no_pads, in0=dst_nat[:, full_tiles, :], scalar=float(FAR),
                                        in1=dst_f[:, full_tiles, :], op0=ALU.is_lt, op1=ALU.mult))
            v.tensor_reduce(span[:, full_tiles:tiles], no_pads, AX.X, ALU.max).then_inc(span_ready, 1)
            v.wait_ge(type8_in, 48)
            v.wait_ge(turned, -(-tiles // 4))
            v.tensor_copy(src_f[:, :, :], type_nat[:, :, :]).then_inc(types_float, 1)
            v.wait_ge(span_copied, 1)
            v.tensor_reduce(group_span_t[:, :], span_t[:, :].rearrange("j (g c) -> j g c", c=GROUP),
                            AX.X, ALU.max).then_inc(groups_ready, 1)

            v.wait_ge(plan_in, 64)
            v.tensor_copy(group_node[:, :], group_base).then_inc(plan_ready, 1)
            done(v.tensor_tensor(fall[:, 0:groups - 1], group_base[:, 0:groups - 1], group_base[:, 1:groups],
                                 ALU.subtract))
            v.tensor_reduce(worst[:, 0:1], group_span, AX.X, ALU.max)
            v.tensor_reduce(worst[:, 1:2], group_reach, AX.X, ALU.max)
            v.tensor_reduce(worst[:, 2:3], fall[:, 0:groups - 1], AX.X, ALU.max)
            for b in range(in_stream):
                g = 2 * ready_after(b) - 2
                ins = v.tensor_scalar(checks[:, 3 + b:4 + b], group_base[:, g:g + 1], float(NB * (b + 1)), None,
                                      ALU.is_lt)
            done(ins)
            v.tensor_scalar(checks[:, 0:1], worst[:, 0:1], float(SPAN), None, ALU.is_ge)
            v.tensor_scalar(checks[:, 1:2], worst[:, 1:2], float(WINDOW - SPAN), None, ALU.is_gt)
            done(v.tensor_scalar(checks[:, 2:3], worst[:, 2:3], 0.0, None, ALU.is_gt))
            done(v.tensor_reduce(fails[:, :], checks[:, :], AX.X, ALU.max))
            v.tensor_copy(general[:, :], fails[:, :]).then_inc(plan_ready, 1)
            v.wait_ge(cols_copied, 2 * -(-tiles // 4))
            done(v.memset(rel_col[:, chunks:tiles * P], -1.0))
            v.wait_ge(sums_zeroed, 3)
            v.wait_ge(plan_ready, 2)

            v.wait_ge(cols_copied, 3 * -(-tiles // 4))

            def for_layer_1():
                v.wait_ge(type64_in, 48)
                v.tensor_copy(src_f[:, :, :].bitcast(BF16)[:, :, 0:P], type_nat[:, :, :]).then_inc(types64_float, 1)
                v.wait_ge(w_in, 16 * 7)
                v.tensor_copy(comp_part[:, 0, :], comp[:, :]).then_inc(comp_step, 1)
                v.wait_ge(comp_step, 1)
                v.tensor_tensor(comp_left[:, 0, :], comp[:, :], comp_part[:, 0, :], ALU.subtract
                                ).then_inc(comp_step, 1)
                v.wait_ge(comp_step, 2)
                v.tensor_copy(comp_part[:, 1, :], comp_left[:, 0, :]).then_inc(comp_step, 1)
                v.wait_ge(comp_step, 3)
                v.tensor_tensor(comp_left[:, 1, :], comp_left[:, 0, :], comp_part[:, 1, :], ALU.subtract
                                ).then_inc(comp_step, 1)
                v.wait_ge(comp_step, 4)
                v.tensor_copy(comp_part[:, 2, :], comp_left[:, 1, :]).then_inc(comp_ready, 1)
                v.tensor_scalar(src_nat[:, :, :], dst_nat[:, :, :], dump, None, ALU.min).then_inc(dst_clamped, 1)

            def along_chunks(col, g, n):
                return col[:, bass.ds(g * GROUP, GROUP)].unsqueeze(2).to_broadcast([P, GROUP, n])

            def counting(n):
                return iota_f[:, 0:n].unsqueeze(1).to_broadcast([P, GROUP, n])

            def spot_types(g):
                v.wait_ge(types_spread, g + 1)
                for b in range(2):
                    ins = v.tensor_scalar(type_hot[:, b * BANK:(b + 1) * BANK], deg_ps[b][:, :], lane_f[:, 0:1],
                                          None, ALU.is_equal)
                ins.then_inc(type_hot_ready, 1)

            for l in range(2):
                r = fan[l]
                def make_coef(g, s):
                    if l == 0:
                        return v.tensor_tensor(coef[s][:, :, 0:r], counting(r), along_chunks(type_col, g, r),
                                               ALU.is_equal)
                    v.wait_ge(coef_summed, g + 1)
                    return v.tensor_tensor(coef[s][:, :, :],
                                           coef_ps[:, 0:GROUP * r].rearrange("p (c r) -> p c r", r=r),
                                           along_chunks(weight_col, g, r), ALU.mult)

                def select(g, s):
                    if not (known(g) and g < 2):
                        v.wait_ge(sums_done[l], g - 1)
                    make_coef(g, s).then_inc(hots_ready[l], 1)
                    v.tensor_tensor(onehot[s][:, :, :], counting(SPAN), along_chunks(rel_col, g, SPAN),
                                    ALU.is_equal).then_inc(hots_ready[l], 1)
                    v.wait_ge(hots_ready[l], 2 * g + 2)
                    v.tensor_tensor(
                        sel[s][:, 0:GROUP * SPAN * r].rearrange("p (c w r) -> p c w r", w=SPAN, r=r),
                        onehot[s][:, :, :].unsqueeze(3).to_broadcast([P, GROUP, SPAN, r]),
                        coef[s][:, :, 0:r].unsqueeze(2).to_broadcast([P, GROUP, SPAN, r]),
                        ALU.mult).then_inc(sel_ready[l], 1)

                def add(g, s, k):
                    node = v.value_load(group_node[0:1, bass.ds(g, 1)], min_val=0, max_val=nodes - 1)
                    at = bass.ds(node, WINDOW)
                    v.wait_ge(prod_done[l], k + 1)
                    if not (known(g) and g < 1):
                        v.wait_ge(added[l], g)
                    v.tensor_tensor(agg[:, at], agg[:, at], products_of(k)[:, s * WINDOW:(s + 1) * WINDOW], ALU.add
                                    ).then_inc(added[l], 1)

                def add_deg(g, s):
                    node = v.value_load(group_node[0:1, bass.ds(g, 1)], min_val=0, max_val=nodes - 1)
                    at = bass.ds(node, WINDOW)
                    v.wait_ge(deg_summed, g + 1)
                    if not (known(g) and g < 1):
                        v.wait_ge(deg_added, g)
                    v.tensor_tensor(deg[:, at], deg[:, at], deg_ps[s][:, 0:WINDOW], ALU.add).then_inc(deg_added, 1)

                def fast():
                    if l:
                        spot_types(0)
                    select(0, 0)
                    if l:
                        spot_types(1)
                        v.memset(agg[:, :], 0.0).then_inc(agg_zeroed, 1)
                        v.wait_ge(agg_zeroed, 1)

                    def step(g, s, k, within=None):
                        if not (known(g) and g == groups - 1):
                            select(g + 1, 1 - s)
                        if within:
                            within[s]()
                        if l and not (known(g) and g >= groups - 2):
                            spot_types(g + 2)
                        if l == 0 and known(g) and g == 1:
                            for_layer_1()
                        if l == 0 and not (known(g) and (g == 0 or g == groups - 1)):
                            add_deg(g - 1, 1 - s)
                        if l == 0 and known(g) and g == groups - 2:
                            for h in range(2):
                                add_deg(g + h, h)
                            invert(bass.ds(in_stream * NB, nodes - in_stream * NB), 3 * in_stream, groups)
                        if s == 1 and not (known(k) and k == 0):
                            for h in range(2):
                                add(2 * (k - 1) + h, h, k - 1)

                    def mean_of(b, n):
                        if l == 0:
                            mean(b, n, 2 * ready_after(b) - 2)
                    stream(v, step, node_parts, lambda: scale(in_stream - 1, 0, NB), mean_of)
                    for h in range(2):
                        add(groups - 2 + h, h, pairs - 1)
                    if l == 0:
                        v.wait_ge(added[l], groups)
                        v.wait_ge(mean_step[l], 3 * in_stream + 2)
                        for b, s, k, n, ps, col in last_batches:
                            v.tensor_tensor(agg[:, span_of(b, n)], agg[:, span_of(b, n)], deg[:, span_of(b, n)],
                                            ALU.mult).then_inc(mean_step[l], 1)
                    for b, s, k, n, ps, col in last_batches:
                        residual(b, s, n, ps)
                    for b, s, k, n, ps, col in last_batches:
                        scale(b, s, n)

                def general_path():
                    if l:
                        v.memset(agg[:, :], 0.0).then_inc(agg_zeroed, 1)
                        v.wait_ge(agg_zeroed, 1)
                    else:
                        for_layer_1()
                    v.sem_inc(g_added[l], 1)
                    v.wait_ge(dst_out, 16)
                    with v.Fori(0, groups) as g:
                        if l:
                            spot_types(g)
                        make_coef(g, 0).then_inc(g_coef[l], 1)
                        v.wait_ge(g_coef[l], g + 1)
                        v.sem_inc(vector_paced, 1)
                        with v.Fori(0, GROUP) as i:
                            for h in range(2):
                                u = (g * GROUP + i) * 2 + h
                                v.wait_ge(g_sums[l], u + 1)
                                v.tensor_tensor(
                                    sel[0][:, 0:HALF * r].rearrange("p (w r) -> p w r", r=r),
                                    ident[:, h * HALF:(h + 1) * HALF].unsqueeze(2).to_broadcast([P, HALF, r]),
                                    coef[0][:, bass.ds(i, 1), 0:r].to_broadcast([P, HALF, r]),
                                    ALU.mult).then_inc(g_sel[l], 1)
                                v.wait_ge(g_prod[l], u + 1)
                                v.sem_inc(vector_paced, 1)
                                v.drain()
                                with v.Fori(0, HALF) as w:
                                    edge = bass.ds(u * HALF + w, 1)
                                    node = v.value_load(dst_lin[edge].rearrange("(o e) -> o e", o=1),
                                                        min_val=0, max_val=dump)
                                    at = bass.ds(node, 1)
                                    v.tensor_tensor(agg[:, at], agg[:, at], prod_ps[:, bass.ds(w, 1)], ALU.add)
                                    if l == 0:
                                        v.tensor_scalar(deg[:, at], deg[:, at], 1.0, None, ALU.add)
                                    v.drain()
                                v.sem_inc(g_added[l], 1)

                    v.drain().then_inc(stream_done[l], 1)
                    v.wait_ge(stream_done[l], 1)
                    v.sem_inc(vector_paced, 1)

                    def both(b, s, k, n):
                        if l == 0:
                            mean(b, n, None)
                        node_turn(b, s, k, n)
                        node_end(b, s, k, n)
                    over_batches(v, (both,))

                def invert(at, steps, groups_added):
                    if groups_added is not None:
                        v.wait_ge(deg_added, groups_added)
                        v.sem_inc(vector_paced, 1)
                    v.tensor_scalar(deg[:, at], deg[:, at], 1.0, None, ALU.max).then_inc(mean_step[l], 1)
                    v.wait_ge(mean_step[l], steps + 1)
                    v.sem_inc(vector_paced, 1)
                    v.reciprocal(deg[:, at], deg[:, at]).then_inc(mean_step[l], 1)

                def mean(b, n, groups_added):
                    at = span_of(b, n)
                    invert(at, 3 * b, groups_added)
                    if groups_added is not None:
                        v.wait_ge(added[l], groups_added)
                    v.wait_ge(mean_step[l], 3 * b + 2)
                    v.tensor_tensor(agg[:, at], agg[:, at], deg[:, at], ALU.mult).then_inc(mean_step[l], 1)

                def residual(b, s, n, ps=prod_ps):
                    parts = parts_of(n)
                    m, c = min(n, P), len(parts)
                    v.wait_ge(act_turned[l], b + 1)
                    if not (known(b) and b < 2):
                        v.wait_ge(normed[l], b - 1)
                    v.tensor_tensor(y[s][0:m, 0:c, :], ps[0:m, 0:c * P].rearrange("p (c f) -> p c f", f=P),
                                    x_in[s][0:m, 0:c, :], ALU.add).then_inc(y_ready[l], 1)
                    v.wait_ge(y_ready[l], b + 1)
                    for j, _ in parts:
                        ins = v.bn_stats(stats[s][0:m, j, :], y[s][0:m, j, :])
                    ins.then_inc(stats_ready[l], 1)
                    v.wait_ge(stats_ready[l], b + 1)
                    v.sem_inc(vector_paced, 1)
                    for j, _ in parts:
                        ins = v.bn_aggr(moments[s][0:m, j, :], stats[s][0:m, j, :])
                    ins.then_inc(moments_ready[l], 1)

                def scale(b, s, n):
                    m, c = min(n, P), len(parts_of(n))
                    v.wait_ge(std_ready[l], b + 1)
                    v.reciprocal(rstd[s][0:m, 0:c], std[s][0:m, 0:c]).then_inc(inverted[l], 1)
                    v.wait_ge(inverted[l], b + 1)
                    v.scalar_tensor_tensor(out=shift[s][0:m, 0:c], in0=moments[s][0:m, 0:c, 0], scalar=-1.0,
                                           in1=rstd[s][0:m, 0:c], op0=ALU.mult, op1=ALU.mult
                                           ).then_inc(rstd_ready[l], 1)

                def node_turn(b, s, k, n):
                    if not (known(b) and b == 0):
                        scale(b - 1, 1 - s, NB)

                def node_end(b, s, k, n):
                    residual(b, s, n)
                    if n != NB:
                        scale(b, s, n)

                node_parts = (node_turn, lambda b, s, k, n: None, node_end)
                paths(v, fast, general_path)


_INS = ["x", "src", "dst", "edge_type_64", "edge_type_8", "edge_weight1", "L0_gnn_W_rel", "L0_gnn_W_self_w",
        "L0_gnn_W_self_b", "L1_gnn_weight", "L1_gnn_w_comp", "L1_gnn_h_bias", "L1_gnn_loop_weight"]


def kernel(**inputs):
    import numpy as np
    import concourse.bacc as bacc
    from concourse.bass_utils import run_bass_kernel_spmd

    nc = bacc.Bacc("TRN2", target_bir_lowering=False, num_devices=1)
    arrays = {f"{name}_dram": np.ascontiguousarray(inputs[name]) for name in _INS}
    args = [nc.dram_tensor(n, a.shape, mybir.dt.from_np(a.dtype), kind="ExternalInput").ap()
            for n, a in arrays.items()]
    out = nc.dram_tensor("out_dram", inputs["x"].shape, F32, kind="ExternalOutput").ap()
    two_layer_gnn(nc, *args, out)
    result = run_bass_kernel_spmd(nc, [arrays], core_ids=[0])
    return result.results[0]["out_dram"]
```
